# Optimizing a Trainium2 kernel written in Bass

```python
import numpy as np
import jax
import jax.numpy as jnp

def _softmax(x, axis=-1):
    return jax.nn.softmax(x, axis=axis)

def _gelu(x):
    return jax.nn.gelu(x, approximate=True)

def _silu(x):
    return jax.nn.silu(x)

def _sigmoid(x):
    return jax.nn.sigmoid(x)

def _layernorm(x, axis=-1, eps=1e-05):
    m = jnp.mean(x, axis=axis, keepdims=True)
    v = jnp.var(x, axis=axis, keepdims=True)
    return (x - m) / jnp.sqrt(v + eps)

def _scatter_add(tgt, idx, src, axis=0):
    return tgt.at[idx].add(src)

def _segment_sum(src, seg, n):
    return jax.ops.segment_sum(src, seg, n)
kernel_name = 'mk_vit_tower_d1_tok_img768_r4_45f281'

def setup_inputs(seed: int=0):
    np.random.seed(seed)
    _w = jnp.asarray

    def _rec_inputs():
        import jax
        import jax.numpy as jnp
        _rk = jax.random.key(seed)
        x = -0.000356955 + 1 * jax.random.normal(jax.random.fold_in(_rk, 1), (32, 3, 64, 64), jnp.float32)
        return x
    x = _rec_inputs()

    def _L0_tok_setup():
        import jax, jax.numpy as jnp
        import numpy as np
        PATCH = 16
        EMBED = 192
        IN_DIM = PATCH * PATCH * 3

        def extract_patches(x, p):
            B, C, H, Wd = x.shape
            h, w = (H // p, Wd // p)
            xr = x.reshape(B, C, h, p, w, p)
            xr = xr.transpose(0, 2, 4, 3, 5, 1)
            return xr.reshape(B, h * w, p * p * C)
        key = jax.random.key(seed)
        kx, kw, kb = jax.random.split(key, 3)
        x = jax.random.normal(kx, (128, 3, 224, 224), dtype=jnp.float32)
        bound = 1.0 / np.sqrt(IN_DIM)
        W = jax.random.uniform(kw, (EMBED, IN_DIM), jnp.float32, -bound, bound)
        b = jax.random.uniform(kb, (EMBED,), jnp.float32, -bound, bound)
        return {'x': x, 'W': W, 'b': b}
    _L0_tok_all = _L0_tok_setup()
    _L0_tok_in = {k: v for k, v in _L0_tok_all.items() if k in ('W', 'b')}
    del _L0_tok_all

    def _L0_attn_setup():
        import jax, jax.numpy as jnp
        import numpy as np
        from jax import lax
        D_MODEL = 192
        D_STATE = 16
        D_CONV = 4
        EXPAND = 2
        D_INNER = EXPAND * D_MODEL
        N = D_STATE // 2
        B_SZ = 8
        SEQ_L = 1024
        key = jax.random.key(seed)
        ks = jax.random.split(key, 8)
        s = 0.02
        return {'x': jax.random.normal(ks[0], (B_SZ, SEQ_L, D_MODEL), jnp.float32), 'W_in': jax.random.normal(ks[1], (D_MODEL, 2 * D_INNER), jnp.float32) * s, 'b_in': jnp.zeros((2 * D_INNER,), jnp.float32), 'conv_w': jax.random.normal(ks[2], (D_INNER, 1, D_CONV), jnp.float32) * s, 'conv_b': jnp.zeros((D_INNER,), jnp.float32), 'W_x': jax.random.normal(ks[3], (D_INNER, 2 * D_STATE), jnp.float32) * s, 'b_x': jnp.zeros((2 * D_STATE,), jnp.float32), 'W_dt': jax.random.normal(ks[4], (D_INNER, D_INNER), jnp.float32) * s, 'b_dt': jnp.zeros((D_INNER,), jnp.float32), 'W_out': jax.random.normal(ks[5], (D_INNER, D_MODEL), jnp.float32) * s, 'b_out': jnp.zeros((D_MODEL,), jnp.float32)}
    _L0_attn_all = _L0_attn_setup()
    _L0_attn_in = {k: v for k, v in _L0_attn_all.items() if k in ('W_in', 'b_in', 'conv_w', 'conv_b', 'W_x', 'b_x', 'W_dt', 'b_dt', 'W_out', 'b_out')}
    del _L0_attn_all

    def _L0_ffn_setup():
        import math
        import jax, jax.numpy as jnp
        import numpy as np
        N_HEAD = 12
        N_EXP = 8
        TOP_K = 2
        TRAIN_CAPACITY = 1.25
        MIN_CAPACITY = 4
        LN_EPS = 1e-05
        NEG_INF = -1e+30

        def _layer_norm(x, w, b):
            mu = jnp.mean(x, axis=-1, keepdims=True)
            var = jnp.var(x, axis=-1, keepdims=True)
            return (x - mu) * jax.lax.rsqrt(var + LN_EPS) * w + b

        def _attention(x, qkv_w, qkv_b, proj_w, proj_b):
            B, T, C = x.shape
            H, D = (N_HEAD, C // N_HEAD)
            qkv = x @ qkv_w + qkv_b
            q, k, v = jnp.split(qkv, 3, axis=-1)
            q = q.reshape(B, T, H, D).transpose(0, 2, 1, 3)
            k = k.reshape(B, T, H, D).transpose(0, 2, 1, 3)
            v = v.reshape(B, T, H, D).transpose(0, 2, 1, 3)
            scores = jnp.einsum('bhqd,bhkd->bhqk', q, k) / math.sqrt(D)
            causal = jnp.tril(jnp.ones((T, T), bool))
            scores = jnp.where(causal, scores, NEG_INF)
            attn = jax.nn.softmax(scores, axis=-1)
            y = jnp.einsum('bhqk,bhkd->bhqd', attn, v)
            y = y.transpose(0, 2, 1, 3).reshape(B, T, C)
            return y @ proj_w + proj_b

        def _moe(x, w_g, fc_w, fc_b, pj_w, pj_b):
            B, T, C = x.shape
            N, E, K = (B * T, N_EXP, TOP_K)
            cap = int(math.floor(K * TRAIN_CAPACITY * N / E))
            cap += cap % 2
            cap = max(cap, MIN_CAPACITY)
            logits = (x @ w_g).reshape(N, E)
            _, topk_idx = jax.lax.top_k(logits, K)
            hot = jax.nn.one_hot(topk_idx, E, dtype=jnp.int32)
            sel = hot.sum(axis=1) > 0
            router_probs = jax.nn.softmax(jnp.where(sel, logits, NEG_INF), axis=-1)
            exp_mask = hot.transpose(1, 0, 2)
            exp_rank = jnp.cumsum(exp_mask.reshape(K * N, E), axis=0) - 1
            exp_rank = exp_rank.reshape(K, N, E)
            exp_mask = exp_mask * (exp_rank < cap).astype(jnp.int32)
            exp_rank = jnp.sum(exp_mask * exp_rank, axis=-1)
            exp_weights = exp_mask.astype(x.dtype) * router_probs[None]
            rank_sc = jax.nn.one_hot(exp_rank, cap, dtype=x.dtype)
            cb_weight = jnp.einsum('kne,knc->nec', exp_weights, rank_sc)
            sec_mask = (cb_weight != 0).astype(x.dtype)
            xf = x.reshape(N, C)
            xb = jnp.einsum('nec,nd->ecd', sec_mask, xf)
            h = jax.nn.gelu(jnp.einsum('ecd,edf->ecf', xb, fc_w) + fc_b, approximate=False)
            out = jnp.einsum('ecf,efd->ecd', h, pj_w) + pj_b
            y = jnp.einsum('nec,ecd->nd', cb_weight, out)
            return y.reshape(B, T, C)
        key = jax.random.key(seed)
        ks = jax.random.split(key, 12)
        B, T, C = (4, 256, 192)
        E, F = (N_EXP, 4 * C)
        s = 0.02
        return {'x': jax.random.normal(ks[0], (B, T, C), jnp.float32), 'ln1_w': jnp.ones((C,), jnp.float32), 'ln1_b': jnp.zeros((C,), jnp.float32), 'ln2_w': jnp.ones((C,), jnp.float32), 'ln2_b': jnp.zeros((C,), jnp.float32), 'attn_qkv_w': jax.random.normal(ks[1], (C, 3 * C), jnp.float32) * s, 'attn_qkv_b': jnp.zeros((3 * C,), jnp.float32), 'attn_proj_w': jax.random.normal(ks[2], (C, C), jnp.float32) * s, 'attn_proj_b': jnp.zeros((C,), jnp.float32), 'w_g': jax.random.normal(ks[3], (C, E), jnp.float32) * s, 'exp_fc_w': jax.random.normal(ks[4], (E, C, F), jnp.float32) * s, 'exp_fc_b': jnp.zeros((E, 1, F), jnp.float32), 'exp_proj_w': jax.random.normal(ks[5], (E, F, C), jnp.float32) * s, 'exp_proj_b': jnp.zeros((E, 1, C), jnp.float32)}
    _L0_ffn_all = _L0_ffn_setup()
    _L0_ffn_in = {k: v for k, v in _L0_ffn_all.items() if k in ('ln1_w', 'ln1_b', 'ln2_w', 'ln2_b', 'attn_qkv_w', 'attn_qkv_b', 'attn_proj_w', 'attn_proj_b', 'w_g', 'exp_fc_w', 'exp_fc_b', 'exp_proj_w', 'exp_proj_b')}
    del _L0_ffn_all
    return {'x': x, 'L0_tok_W': _L0_tok_in['W'], 'L0_tok_b': _L0_tok_in['b'], 'L0_attn_W_in': _L0_attn_in['W_in'], 'L0_attn_b_in': _L0_attn_in['b_in'], 'L0_attn_conv_w': _L0_attn_in['conv_w'], 'L0_attn_conv_b': _L0_attn_in['conv_b'], 'L0_attn_W_x': _L0_attn_in['W_x'], 'L0_attn_b_x': _L0_attn_in['b_x'], 'L0_attn_W_dt': _L0_attn_in['W_dt'], 'L0_attn_b_dt': _L0_attn_in['b_dt'], 'L0_attn_W_out': _L0_attn_in['W_out'], 'L0_attn_b_out': _L0_attn_in['b_out'], 'L0_ffn_ln1_w': _L0_ffn_in['ln1_w'], 'L0_ffn_ln1_b': _L0_ffn_in['ln1_b'], 'L0_ffn_ln2_w': _L0_ffn_in['ln2_w'], 'L0_ffn_ln2_b': _L0_ffn_in['ln2_b'], 'L0_ffn_attn_qkv_w': _L0_ffn_in['attn_qkv_w'], 'L0_ffn_attn_qkv_b': _L0_ffn_in['attn_qkv_b'], 'L0_ffn_attn_proj_w': _L0_ffn_in['attn_proj_w'], 'L0_ffn_attn_proj_b': _L0_ffn_in['attn_proj_b'], 'L0_ffn_w_g': _L0_ffn_in['w_g'], 'L0_ffn_exp_fc_w': _L0_ffn_in['exp_fc_w'], 'L0_ffn_exp_fc_b': _L0_ffn_in['exp_fc_b'], 'L0_ffn_exp_proj_w': _L0_ffn_in['exp_proj_w'], 'L0_ffn_exp_proj_b': _L0_ffn_in['exp_proj_b']}

def reference(x, L0_tok_W, L0_tok_b, L0_attn_W_in, L0_attn_b_in, L0_attn_conv_w, L0_attn_conv_b, L0_attn_W_x, L0_attn_b_x, L0_attn_W_dt, L0_attn_b_dt, L0_attn_W_out, L0_attn_b_out, L0_ffn_ln1_w, L0_ffn_ln1_b, L0_ffn_ln2_w, L0_ffn_ln2_b, L0_ffn_attn_qkv_w, L0_ffn_attn_qkv_b, L0_ffn_attn_proj_w, L0_ffn_attn_proj_b, L0_ffn_w_g, L0_ffn_exp_fc_w, L0_ffn_exp_fc_b, L0_ffn_exp_proj_w, L0_ffn_exp_proj_b):
    import jax
    import jax.numpy as jnp

    def _L0_tok_ref(x, W, b):
        import jax, jax.numpy as jnp
        import numpy as np
        PATCH = 16
        EMBED = 192
        IN_DIM = PATCH * PATCH * 3

        def extract_patches(x, p):
            B, C, H, Wd = x.shape
            h, w = (H // p, Wd // p)
            xr = x.reshape(B, C, h, p, w, p)
            xr = xr.transpose(0, 2, 4, 3, 5, 1)
            return xr.reshape(B, h * w, p * p * C)
        patches = extract_patches(x, PATCH)
        return jnp.einsum('bnd,ed->bne', patches, W) + b

    def _L0_attn_ref(x, W_in, b_in, conv_w, conv_b, W_x, b_x, W_dt, b_dt, W_out, b_out):
        import jax, jax.numpy as jnp
        import numpy as np
        from jax import lax
        D_MODEL = 192
        D_STATE = 16
        D_CONV = 4
        EXPAND = 2
        D_INNER = EXPAND * D_MODEL
        N = D_STATE // 2
        B_SZ = 8
        SEQ_L = 1024
        B, L, _ = x.shape
        xz = x @ W_in + b_in
        xc, z = jnp.split(xz, 2, axis=-1)
        xt = jnp.transpose(xc, (0, 2, 1))
        xt = lax.conv_general_dilated(xt, conv_w, window_strides=(1,), padding=((D_CONV - 1, 0),), dimension_numbers=('NCH', 'OIH', 'NCH'), feature_group_count=D_INNER)
        xt = xt + conv_b[None, :, None]
        xc = jax.nn.silu(jnp.transpose(xt, (0, 2, 1)))
        delta = jax.nn.softplus(xc @ W_dt + b_dt)[..., :N]
        BC = (xc @ W_x + b_x)[..., D_STATE:]
        Bm, Cm = (BC[..., :N], BC[..., N:])
        decay = jnp.exp(-delta)
        xn = xc[..., :N]

        def step(h, ins):
            d_t, B_t, C_t, x_t = ins
            h = h * d_t[:, None, :] + B_t[:, None, :] * x_t[:, :, None]
            y = jnp.einsum('bj,bij->bi', C_t, h)
            return (h, y)
        tm = lambda a: jnp.transpose(a, (1, 0, 2))
        h0 = jnp.zeros((B, N, N), x.dtype)
        _, ys = lax.scan(step, h0, (tm(decay), tm(Bm), tm(Cm), tm(xn)))
        ys = jnp.transpose(ys, (1, 0, 2))
        ssm_out = jnp.pad(ys, ((0, 0), (0, 0), (0, D_INNER - N)))
        out = ssm_out * jax.nn.silu(z) @ W_out + b_out
        return out

    def _L0_ffn_ref(x, ln1_w, ln1_b, ln2_w, ln2_b, attn_qkv_w, attn_qkv_b, attn_proj_w, attn_proj_b, w_g, exp_fc_w, exp_fc_b, exp_proj_w, exp_proj_b):
        import math
        import jax, jax.numpy as jnp
        import numpy as np
        N_HEAD = 12
        N_EXP = 8
        TOP_K = 2
        TRAIN_CAPACITY = 1.25
        MIN_CAPACITY = 4
        LN_EPS = 1e-05
        NEG_INF = -1e+30

        def _layer_norm(x, w, b):
            mu = jnp.mean(x, axis=-1, keepdims=True)
            var = jnp.var(x, axis=-1, keepdims=True)
            return (x - mu) * jax.lax.rsqrt(var + LN_EPS) * w + b

        def _attention(x, qkv_w, qkv_b, proj_w, proj_b):
            B, T, C = x.shape
            H, D = (N_HEAD, C // N_HEAD)
            qkv = x @ qkv_w + qkv_b
            q, k, v = jnp.split(qkv, 3, axis=-1)
            q = q.reshape(B, T, H, D).transpose(0, 2, 1, 3)
            k = k.reshape(B, T, H, D).transpose(0, 2, 1, 3)
            v = v.reshape(B, T, H, D).transpose(0, 2, 1, 3)
            scores = jnp.einsum('bhqd,bhkd->bhqk', q, k) / math.sqrt(D)
            causal = jnp.tril(jnp.ones((T, T), bool))
            scores = jnp.where(causal, scores, NEG_INF)
            attn = jax.nn.softmax(scores, axis=-1)
            y = jnp.einsum('bhqk,bhkd->bhqd', attn, v)
            y = y.transpose(0, 2, 1, 3).reshape(B, T, C)
            return y @ proj_w + proj_b

        def _moe(x, w_g, fc_w, fc_b, pj_w, pj_b):
            B, T, C = x.shape
            N, E, K = (B * T, N_EXP, TOP_K)
            cap = int(math.floor(K * TRAIN_CAPACITY * N / E))
            cap += cap % 2
            cap = max(cap, MIN_CAPACITY)
            logits = (x @ w_g).reshape(N, E)
            _, topk_idx = jax.lax.top_k(logits, K)
            hot = jax.nn.one_hot(topk_idx, E, dtype=jnp.int32)
            sel = hot.sum(axis=1) > 0
            router_probs = jax.nn.softmax(jnp.where(sel, logits, NEG_INF), axis=-1)
            exp_mask = hot.transpose(1, 0, 2)
            exp_rank = jnp.cumsum(exp_mask.reshape(K * N, E), axis=0) - 1
            exp_rank = exp_rank.reshape(K, N, E)
            exp_mask = exp_mask * (exp_rank < cap).astype(jnp.int32)
            exp_rank = jnp.sum(exp_mask * exp_rank, axis=-1)
            exp_weights = exp_mask.astype(x.dtype) * router_probs[None]
            rank_sc = jax.nn.one_hot(exp_rank, cap, dtype=x.dtype)
            cb_weight = jnp.einsum('kne,knc->nec', exp_weights, rank_sc)
            sec_mask = (cb_weight != 0).astype(x.dtype)
            xf = x.reshape(N, C)
            xb = jnp.einsum('nec,nd->ecd', sec_mask, xf)
            h = jax.nn.gelu(jnp.einsum('ecd,edf->ecf', xb, fc_w) + fc_b, approximate=False)
            out = jnp.einsum('ecf,efd->ecd', h, pj_w) + pj_b
            y = jnp.einsum('nec,ecd->nd', cb_weight, out)
            return y.reshape(B, T, C)
        x = x + _attention(_layer_norm(x, ln1_w, ln1_b), attn_qkv_w, attn_qkv_b, attn_proj_w, attn_proj_b)
        x = x + _moe(_layer_norm(x, ln2_w, ln2_b), w_g, exp_fc_w, exp_fc_b, exp_proj_w, exp_proj_b)
        return x
    h = _L0_tok_ref(x, L0_tok_W, L0_tok_b)
    h = h + _L0_attn_ref(_layernorm(h, axis=-1), L0_attn_W_in, L0_attn_b_in, L0_attn_conv_w, L0_attn_conv_b, L0_attn_W_x, L0_attn_b_x, L0_attn_W_dt, L0_attn_b_dt, L0_attn_W_out, L0_attn_b_out)
    h = h + _L0_ffn_ref(_layernorm(h, axis=-1), L0_ffn_ln1_w, L0_ffn_ln1_b, L0_ffn_ln2_w, L0_ffn_ln2_b, L0_ffn_attn_qkv_w, L0_ffn_attn_qkv_b, L0_ffn_attn_proj_w, L0_ffn_attn_proj_b, L0_ffn_w_g, L0_ffn_exp_fc_w, L0_ffn_exp_fc_b, L0_ffn_exp_proj_w, L0_ffn_exp_proj_b)
    return h

_drawn_inputs = setup_inputs


def setup_inputs(seed=0):
    import zlib

    import numpy as np

    out = dict(_drawn_inputs(seed))
    spreads = {'L0_attn_b_in': (0.0, 0.8),
     'L0_attn_conv_b': (0.0, 0.8),
     'L0_attn_b_x': (0.0, 0.8),
     'L0_attn_b_dt': (0.0, 0.8),
     'L0_attn_b_out': (0.0, 0.8),
     'L0_ffn_ln1_w': (1.0, 0.6),
     'L0_ffn_ln1_b': (0.0, 2.0),
     'L0_ffn_ln2_w': (1.0, 0.6),
     'L0_ffn_ln2_b': (0.0, 2.0),
     'L0_ffn_attn_qkv_b': (0.0, 2.0),
     'L0_ffn_attn_proj_b': (0.0, 0.8),
     'L0_ffn_exp_fc_b': (0.0, 2.0),
     'L0_ffn_exp_proj_b': (0.0, 2.0)}
    factors = {'L0_attn_W_in': 8.0,
     'L0_attn_conv_w': 8.0,
     'L0_attn_W_x': 8.0,
     'L0_attn_W_dt': 8.0,
     'L0_attn_W_out': 8.0,
     'L0_ffn_attn_qkv_w': 8.0,
     'L0_ffn_attn_proj_w': 8.0,
     'L0_ffn_w_g': 8.0,
     'L0_ffn_exp_fc_w': 8.0,
     'L0_ffn_exp_proj_w': 8.0}
    for name, (base, spread) in spreads.items():
        noise = np.random.default_rng([zlib.crc32(name.encode()), seed]).standard_normal(out[name].shape)
        drawn = base * np.exp(spread * noise) if base else spread * noise
        out[name] = jnp.asarray(drawn.astype(out[name].dtype))
    for name, factor in factors.items():
        out[name] = (out[name] * factor).astype(out[name].dtype)
    return out
```

```python
from contextlib import ExitStack

import numpy as np

import concourse.bass as bass
from concourse import mybir
from concourse.alu_op_type import AluOpType as ALU

F32 = mybir.dt.float32
BF16 = mybir.dt.bfloat16
I32 = mybir.dt.int32
ACT = mybir.ActivationFunctionType
AX_X = mybir.AxisListType.X

P = 128
B, T = 32, 16
N = B * T
NT = N // P
BT = P // T
D = 192
HALF = D // 2
PIX = 768
KP = PIX // P
PIECES = 3
INNER = 384
KI = INNER // P
S = 8
SS = S * S
TAPS = 4
HEADS, DH = 12, 16
HH = HEADS // 2
E, TOPK = 8, 2
CAP = 160
CAP += CAP % 2
assert CAP == int(TOPK * 1.25 * N / E)
SLOTS = E * CAP
M2 = CAP // 2
F = 768
KF = F // P
J = TOPK * NT
EPS = 1e-5
NEG = -1.0e30
ZERO = 240
WIN = INNER + S

PP_BIN, PP_CW, PP_CB, PP_FCB = 0, KI, KI + KI * TAPS, 2 * KI + KI * TAPS
PP_W = PP_FCB + E * KF
QP_L1W, QP_L1B, QP_L2W, QP_L2B, QP_QB, QP_KB, QP_W = 0, 2, 4, 6, 8, 10, 12
SP_DT, SP_C, SP_Z, SP_W = 0, 1, 2, 3
C_ID, C_TRI, C_ONE = 0, P, 2 * P
C_CM = 3 * P
C_HM = C_CM + T
C_BM = C_HM + HH
C_REV = C_BM + BT
C_E160 = C_REV + NT * E
C_TRASH = C_E160 + J * E
C_SEL = C_TRASH + J
C_HALF = C_SEL + P
C_W = C_HALF + NT
C_BF = C_CM + T


def constants():
    c = np.zeros((P, C_W), np.float32)
    p = np.arange(P)
    c[:, C_ID:C_ID + P] = np.eye(P)
    c[:, C_TRI:C_TRI + P] = p[:, None] < p[None, :]
    c[:, C_ONE:C_ONE + P] = 1.0
    c[:HALF, C_CM:C_CM + T] = np.where(np.arange(T)[None, :] <= (p[:HALF] % T)[:, None], 0.0, NEG)
    c[:HALF, C_HM:C_HM + HH] = (p[:HALF, None] // DH == np.arange(HH)[None, :]) * DH ** -0.5
    c[:, C_BM:C_BM + BT] = p[:, None] // T == np.arange(BT)[None, :]
    c[:, C_REV:C_REV + NT * E] = np.tile(E - np.arange(E), NT)
    c[:, C_E160:C_E160 + J * E] = np.tile(np.arange(E) * CAP, J)
    c[:, C_TRASH:C_TRASH + J] = SLOTS + np.arange(J)[None, :] * P + p[:, None]
    c[:S, C_SEL + SS:C_SEL + 2 * SS] = np.arange(SS)[None, :] // S == np.arange(S)[:, None]
    c[:, C_HALF:C_HALF + NT] = -0.5
    return c


def vit_block(nc, patches, tok_w, w_in, w_z, w_state, w_out, qkv_w, proj_w, gate_w, fc_w, pj_w,
              pp, qp, sp_par, rows, pj_b, consts, out):
    ctx = ExitStack()
    with ctx:
        def sb(name, shape, dt=F32):
            return ctx.enter_context(nc.sbuf_tensor(name, shape, dt))

        def sem(name):
            return ctx.enter_context(nc.semaphore(name))

        slot_in = nc.dram_tensor("slot_in", (SLOTS + TOPK * N, D), F32).ap()
        slot_out = nc.dram_tensor("slot_out", (SLOTS, D), F32).ap()

        bank = [ctx.enter_context(nc.psum_tensor(f"bank{i}", [P, 512], F32)) for i in range(8)]

        cst = sb("cst", [P, C_W])
        cstb = sb("cstb", [P, C_BF], BF16)
        ppt = sb("ppt", [P, PP_W])
        qpt = sb("qpt", [HALF, QP_W])
        spt = sb("spt", [P, SP_W])
        row = sb("row", [P, 4, D])
        pjb = sb("pjb", [M2, E, D])
        pat = sb("pat", [P, KP, N])
        tokw = sb("tokw", [P, KP, D])
        win = sb("win", [HALF, 2, INNER])
        winz = sb("winz", [HALF, 2, SS])
        wst = sb("wst", [P, KI, 3 * SS])
        wout = sb("wout", [SS, D])
        qkvw = sb("qkvw", [HALF, 2, 3 * D])
        projw = sb("projw", [HALF, 2, D])
        gatew = sb("gatew", [HALF, 2, E])
        fcw = sb("fcw", [HALF, E, 2, F])
        pjw = sb("pjw", [P, E, KF, D])
        zeros = sb("zeros", [P, ZERO])

        h = sb("h", [P, NT, D])
        h2 = sb("h2", [P, NT, D])
        xh = sb("xh", [P, NT, D])
        xp = sb("xp", [P, NT, D])
        x1 = sb("x1", [P, NT, D])
        st = sb("st", [P, NT, 6])
        mv = sb("mv", [P, NT, 2])
        rstd = sb("rstd", [P, NT])
        xT = sb("xT", [HALF, 2, N])
        conv = sb("conv", [P, 2, KI, N])
        xc = sb("xc", [P, KI, N])
        ndtb = sb("ndtb", [SS, 1])
        sz = sb("sz", [SS, N])
        xrep = sb("xrep", [P, N])
        decay = sb("decay", [SS, N])
        bx = sb("bx", [SS, N])
        cz = sb("cz", [SS, N])
        hs = conv[0:SS, 0, 0, :]
        qbm = sb("qbm", [HALF, HH])
        kT = sb("kT", [HALF, 2, N])
        big = sb("big", [P, HEADS * N])
        v = sb("v", [P, NT, HEADS, DH + 1])
        nmax = sb("nmax", [HALF, 2, B])
        prob = xc[0:HALF, 0:2, :]
        den = sb("den", [P, NT, HEADS])
        o = tokw[:, 0:NT, :]
        oT = kT
        lg = sb("lg", [P, NT, E])
        lg2 = sb("lg2", [P, NT, E])
        cand = sb("cand", [P, NT, E])
        top = sb("top", [P, J])
        first = sb("first", [P, J])
        hot = sb("hot", [P, J, E])
        hotb = sb("hotb", [P, J, E], BF16)
        gap = sb("gap", [P, NT])
        wgt = sb("wgt", [P, J])
        off = sb("off", [P, J, E])
        offs = sb("offs", [P, J])
        pos = sb("pos", [P, J, E])
        slot = sb("slot", [P, J])
        rank = sb("rank", [P, J])
        kept = sb("kept", [P, J])
        dst = sb("dst", [P, J])
        put = sb("put", [P, J], I32)
        get = sb("get", [P, J], I32)
        hid = big[:, 0:2 * KF * CAP].rearrange("p (b f s) -> p b f s", b=2, f=KF)
        got = big[:, 2 * KF * CAP:2 * KF * CAP + J * D].rearrange("p (j d) -> p j d", j=J)
        xbT = big[0:HALF, HEADS * N - 4 * CAP:HEADS * N].rearrange("p (b c s) -> p b c s", b=2, c=2)

        slot_rows = pat[0:M2, :, :].rearrange("p a b -> p (a b)")[:, 0:2 * E * D].rearrange("p (n d) -> p n d", d=D)
        y_rows = conv[0:M2, :, :, :].rearrange("p x a b -> p (x a b)")[:, 0:2 * E * D].rearrange(
            "p (n d) -> p n d", d=D)
        qx = big[0:HALF, :].rearrange("p (c b h q) -> p c b h q", c=2, b=B, h=HH)
        px = big[:, :].rearrange("p (t h b q) -> p t h b q", t=NT, h=HEADS, b=BT)
        ident = cst[:, C_ID:C_ID + P]
        hmask = cst[0:HALF, C_HM:C_HM + HH]
        bmask = cst[:, C_BM:C_BM + BT]

        in_tok = [sem(f"in_tok{i}") for i in range(PIECES)]
        in_cst, in_small, in_ssm, in_rows, in_attn, in_zero = (sem(n) for n in (
            "in_cst", "in_small", "in_ssm", "in_rows", "in_attn", "in_zero"))
        in_fc = [sem(f"in_fc{e}") for e in range(E)]
        in_pj = [sem(f"in_pj{e}") for e in range(E)]
        zeros_ready, zero_rows = sem("zeros_ready"), sem("zero_rows")
        cstb_ready = sem("cstb_ready")
        tok_acc, ln_T, xz_acc, st_acc, ssm_acc, qk_acc, v_acc, s_acc, p_T, o_acc, o_T, x1_acc = (sem(n) for n in (
            "tok_acc", "ln_T", "xz_acc", "st_acc", "ssm_acc", "qk_acc", "v_acc", "s_acc", "p_T", "o_acc", "o_T",
            "x1_acc"))
        lg_acc, pos_acc, xb_T, fc_acc, pj_acc = (sem(n) for n in ("lg_acc", "pos_acc", "xb_T", "fc_acc", "pj_acc"))
        ln_ready, xT_act, xT_dve, conv_in, conv_out, xc_ready, small_ready = (sem(n) for n in (
            "ln_ready", "xT_act", "xT_dve", "conv_in", "conv_out", "xc_ready", "small_ready"))
        sz_ready, xrep_ready, decay_ready, g_ready, hb_ready, h_ready = (sem(n) for n in (
            "sz_ready", "xrep_ready", "decay_ready", "g_ready", "hb_ready", "h_ready"))
        qx_act, qx_dve, kT_ready, v_ready, shifted, prob_ready, px_ready, o_ready, oT_act, oT_dve = (
            sem(n) for n in ("qx_act", "qx_dve", "kT_ready", "v_ready", "shifted", "prob_ready", "px_ready",
                             "o_ready", "oT_act", "oT_dve"))
        xpb_ready, h2_ready, base_ready, gap_ready, wgt_ready, hotb_ready, put_ready, get_ready = (sem(n) for n in (
            "xpb_ready", "h2_ready", "base_ready", "gap_ready", "wgt_ready", "hotb_ready", "put_ready",
            "get_ready"))
        scattered, xbT_ready, hid_ready, y_ready, y_stored, res_ready, stored = (
            sem(n) for n in ("scattered", "xbT_ready", "hid_ready", "y_ready", "y_stored", "res_ready", "stored"))
        slot_loaded = [sem(f"slot_loaded{i}") for i in range(2)]
        gathered = [sem(f"gathered{t}") for t in range(NT)]
        dve_step, pool_step = sem("dve_step"), sem("pool_step")
        ones_ready, var_ready, rstd_ready = sem("ones_ready"), sem("var_ready"), sem("rstd_ready")

        block = ctx.enter_context(nc.Block())

        @block.sync
        def _(sync):
            for i in range(PIECES):
                k = slice(i * KP // PIECES, (i + 1) * KP // PIECES)
                sync.dma_start(pat[:, k, :], patches[:, k, :]).then_inc(in_tok[i], 16)
                sync.dma_start(tokw[:, k, :], tok_w[:, k, :]).then_inc(in_tok[i], 16)
            sync.dma_start(win[:], w_in).then_inc(in_ssm, 16)
            sync.dma_start(winz[:], w_z).then_inc(in_ssm, 16)
            sync.dma_start(wst[:], w_state).then_inc(in_ssm, 16)
            sync.dma_start(wout[:], w_out).then_inc(in_ssm, 16)
            sync.dma_start(qkvw[:], qkv_w).then_inc(in_attn, 16)
            sync.dma_start(projw[:], proj_w).then_inc(in_attn, 16)
            sync.dma_start(gatew[:], gate_w).then_inc(in_attn, 16)
            sync.wait_ge(zeros_ready, 1)
            sync.dma_start(slot_in[0:SLOTS, :].rearrange("(p n) d -> p (n d)", p=P).rearrange("p (r z) -> p r z", z=ZERO),
                           zeros[:].unsqueeze(1).to_broadcast([P, SLOTS // P * D // ZERO, ZERO])).then_inc(zero_rows, 16)
            for e in range(E):
                sync.dma_start(fcw[:, e, :, :], fc_w[:, e, :, :]).then_inc(in_fc[e], 16)
                sync.dma_start(pjw[:, e, :, :], pj_w[:, e, :, :]).then_inc(in_pj[e], 16)
            sync.wait_ge(scattered, 16 * J)
            for i in range(2):
                n = slice(i * E, (i + 1) * E)
                sync.dma_start(slot_rows[:, n, :], slot_in[i * SLOTS // 2:(i + 1) * SLOTS // 2, :].rearrange(
                    "(n p) d -> p n d", p=M2)).then_inc(slot_loaded[i], 16)
            for e in range(E):
                sync.wait_ge(y_ready, e + 1)
                sync.dma_start(slot_out[e * CAP:(e + 1) * CAP, :].rearrange("(n p) d -> p n d", p=M2),
                               y_rows[:, 2 * e:2 * e + 2, :]).then_inc(y_stored, 16)
            for t in range(NT):
                sync.wait_ge(res_ready, t + 1)
                sync.dma_start(out[t * P:(t + 1) * P, :], h2[:, t, :]).then_inc(stored, 16)
            sync.wait_ge(stored, 16 * NT)

        @block.gpsimd
        def _(pool):
            steps = [0]

            def step(ins):
                steps[0] += 1
                ins.then_inc(pool_step, 1)
                pool.wait_ge(pool_step, steps[0])

            nc.gpsimd.memset(zeros[:], 0.0).then_inc(zeros_ready, 1)
            nc.gpsimd.memset(v[:, :, :, DH:DH + 1], 1.0).then_inc(ones_ready, 1)

            def rstd_of(n):
                pool.wait_ge(var_ready, n)
                step(nc.gpsimd.tensor_scalar(rstd[:], mv[:, :, 1], EPS, None, ALU.add))
                nc.gpsimd.tensor_tensor(rstd[:], rstd[:], cst[:, C_HALF:C_HALF + NT], ALU.pow).then_inc(rstd_ready, 1)

            pool.wait_ge(in_cst, 16)
            rstd_of(1)
            pool.wait_ge(h_ready, NT)
            pool.wait_ge(in_rows, 16)
            pool.wait_ge(ln_ready, NT)
            nc.gpsimd.tensor_tensor(h[:], h[:], row[:, 1:2, :].to_broadcast([P, NT, D]), ALU.add).then_inc(hb_ready, 1)
            rstd_of(2)
            rstd_of(3)
            pool.wait_ge(ln_ready, 3 * NT)
            nc.gpsimd.tensor_tensor(xp[:], xp[:], row[:, 3:4, :].to_broadcast([P, NT, D]), ALU.add).then_inc(xpb_ready, 1)
            rstd_of(4)
            pool.wait_ge(ln_ready, 4 * NT)
            nc.gpsimd.tensor_tensor(h2[:], h2[:], x1[:], ALU.add).then_inc(base_ready, 1)
            pool.wait_ge(put_ready, 1)
            pool.wait_ge(zero_rows, 16)
            for j in range(J):
                nc.gpsimd.indirect_dma_start(
                    out=slot_in, out_offset=bass.IndirectOffsetOnAxis(ap=put[:, j:j + 1], axis=0),
                    in_=xh[:, j % NT, :], in_offset=None).then_inc(scattered, 16)
            pool.wait_ge(get_ready, 1)
            pool.wait_ge(y_stored, 16 * E)
            for j in [k * NT + t for t in range(NT) for k in range(TOPK)]:
                nc.gpsimd.indirect_dma_start(
                    out=got[:, j, :], out_offset=None, in_=slot_out,
                    in_offset=bass.IndirectOffsetOnAxis(ap=get[:, j:j + 1], axis=0)).then_inc(gathered[j % NT], 16)

        @block.scalar
        def _(act):
            act.dma_start(cst[:], consts).then_inc(in_cst, 16)
            act.dma_start(ppt[:], pp).then_inc(in_small, 16)
            act.dma_start(qpt[:], qp).then_inc(in_small, 16)
            act.dma_start(spt[:], sp_par).then_inc(in_small, 16)
            act.dma_start(row[:], rows.partition_broadcast(P)).then_inc(in_rows, 16)
            act.dma_start(pjb[:], pj_b.partition_broadcast(M2)).then_inc(in_pj[0], 16)
            act.wait_ge(in_cst, 16)
            nc.scalar.activation(cstb[:], cst[:, 0:C_BF], ACT.Copy).then_inc(cstb_ready, 1)

            act.wait_ge(ln_T, 1)
            nc.scalar.activation(xT[:, 0, :], bank[4][0:HALF, :], ACT.Copy).then_inc(xT_act, 1)
            act.wait_ge(in_small, 48)
            for m in range(KI):
                act.wait_ge(xz_acc, m + 1)
                nc.scalar.activation(conv[:, 0, m, :], bank[(6 + m) % 8][:], ACT.Identity,
                                     bias=ppt[:, PP_BIN + m:PP_BIN + m + 1]).then_inc(conv_in, 1)
            act.wait_ge(xz_acc, KI + 1)
            nc.scalar.activation(sz[:], bank[1][0:SS, :], ACT.Silu, bias=spt[0:SS, SP_Z:SP_Z + 1]).then_inc(sz_ready, 1)
            for m in range(KI):
                act.wait_ge(conv_out, m + 1)
                nc.scalar.activation(xc[:, m, :], conv[:, 1, m, :], ACT.Silu,
                                     bias=ppt[:, PP_CB + m:PP_CB + m + 1]).then_inc(xc_ready, 1)
            act.wait_ge(st_acc, 1)
            nc.scalar.activation(xrep[SS:2 * SS, :], bank[4][SS:2 * SS, :], ACT.Copy).then_inc(xrep_ready, 1)
            act.wait_ge(st_acc, 2)
            act.wait_ge(small_ready, 2)
            nc.scalar.activation(decay[:], bank[2][0:SS, :], ACT.Sigmoid, scale=-1.0, bias=ndtb[:]).then_inc(decay_ready, 1)

            act.wait_ge(ln_T, 2)
            nc.scalar.activation(xT[:, 0, :], bank[1][0:HALF, :], ACT.Identity, scale=qpt[:, QP_L1W:QP_L1W + 1],
                                 bias=qpt[:, QP_L1B:QP_L1B + 1]).then_inc(xT_act, 1)
            act.wait_ge(qk_acc, 1)
            act.wait_ge(small_ready, 2)
            for hd in range(HH):
                nc.scalar.activation(qx[:, 0, :, hd, :], bank[3][0:HALF, :].rearrange("p (b q) -> p b q", b=B),
                                     ACT.Identity, scale=hmask[:, hd:hd + 1], bias=qbm[:, hd:hd + 1]).then_inc(qx_act, 1)
            for c in range(2):
                act.wait_ge(qk_acc, c + 3)
                nc.scalar.activation(kT[:, c, :], bank[5 + c][0:HALF, :], ACT.Identity,
                                     bias=qpt[:, QP_KB + c:QP_KB + c + 1]).then_inc(kT_ready, 1)
            for c in range(2):
                act.wait_ge(shifted, c + 1)
                nc.scalar.activation(prob[:, c, :], prob[:, c, :], ACT.Exp).then_inc(prob_ready, 1)
            act.wait_ge(o_T, 1)
            nc.scalar.activation(oT[:, 0, :], bank[3][0:HALF, :], ACT.Copy).then_inc(oT_act, 1)

            act.wait_ge(ln_T, 3)
            nc.scalar.activation(xT[:, 0, :], bank[1][0:HALF, :], ACT.Identity, scale=qpt[:, QP_L2W:QP_L2W + 1],
                                 bias=qpt[:, QP_L2B:QP_L2B + 1]).then_inc(xT_act, 1)
            act.wait_ge(gap_ready, 1)
            for k in range(TOPK):
                nc.scalar.activation(wgt[:, k * NT:(k + 1) * NT], gap[:], ACT.Sigmoid,
                                     scale=(-1.0, 1.0)[k]).then_inc(wgt_ready, 1)
            for e in range(E):
                for m in range(2):
                    act.wait_ge(fc_acc, 2 * e + m + 1)
                    if e >= 2:
                        act.wait_ge(pj_acc, e - 1)
                    for n in range(KF // 2):
                        f = m * KF // 2 + n
                        nc.scalar.activation(
                            hid[:, e % 2, f, :], bank[2 * (e % 2) + m][:, n * CAP:(n + 1) * CAP], ACT.Gelu,
                            bias=ppt[:, PP_FCB + e * KF + f:PP_FCB + e * KF + f + 1]).then_inc(hid_ready, 1)

        @block.tensor
        def _(pe):
            mm = nc.tensor.matmul

            def transpose_rows(t, halves, src):
                for c in range(2):
                    ins = nc.tensor.transpose(halves[c][0:HALF, t * P:(t + 1) * P],
                                              src[:, t, c * HALF:(c + 1) * HALF], ident)
                return ins

            for i in range(PIECES):
                pe.wait_ge(in_tok[i], 32)
                for k in range(i * KP // PIECES, (i + 1) * KP // PIECES):
                    for t in range(NT):
                        ins = mm(bank[t][:, 0:D], pat[:, k, t * P:(t + 1) * P], tokw[:, k, :],
                                 start=(k == 0), stop=(k == KP - 1))
                        if k == KP - 1:
                            ins.then_inc(tok_acc, 1)
            pe.wait_ge(in_cst, 16)
            for t in range(NT):
                pe.wait_ge(ln_ready, t + 1)
                ins = transpose_rows(t, (bank[4], bank[5]), xh)
            ins.then_inc(ln_T, 1)

            pe.wait_ge(in_ssm, 64)
            pe.wait_ge(xT_act, 1)
            pe.wait_ge(xT_dve, 1)
            for m in range(KI):
                for c in range(2):
                    ins = mm(bank[(6 + m) % 8][:], win[:, c, m * P:(m + 1) * P], xT[:, c, :], start=(c == 0), stop=(c == 1))
                ins.then_inc(xz_acc, 1)
            for c in range(2):
                ins = mm(bank[1][0:SS, :], winz[:, c, :], xT[:, c, :], start=(c == 0), stop=(c == 1))
            ins.then_inc(xz_acc, 1)
            pe.wait_ge(xc_ready, 1)
            mm(bank[4][:], cst[0:S, C_SEL:C_SEL + P], xc[0:S, 0, :], start=True, stop=True).then_inc(st_acc, 1)
            for k in range(KI):
                pe.wait_ge(xc_ready, k + 1)
                ins = mm(bank[2][:], wst[:, k, 0:2 * SS], xc[:, k, :], start=(k == 0), stop=(k == KI - 1))
            ins.then_inc(st_acc, 1)
            for k in range(KI):
                ins = mm(bank[3][0:SS, :], wst[:, k, 2 * SS:3 * SS], xc[:, k, :], start=(k == 0), stop=(k == KI - 1))
            ins.then_inc(st_acc, 1)
            pe.wait_ge(g_ready, 1)
            for t in range(NT):
                mm(bank[(5 + t) % 8][:, 0:D], cz[:, t * P:(t + 1) * P], wout[:], start=True, stop=True).then_inc(ssm_acc, 1)

            for t in range(NT):
                pe.wait_ge(ln_ready, 2 * NT + t + 1)
                ins = transpose_rows(t, (bank[1], bank[2]), xh)
            ins.then_inc(ln_T, 1)
            pe.wait_ge(in_attn, 48)
            pe.wait_ge(xT_act, 2)
            pe.wait_ge(xT_dve, 2)
            for kind in range(2):
                for c in range(2):
                    at = kind * D + c * HALF
                    for k in range(2):
                        ins = mm(bank[3 + 2 * kind + c][0:HALF, :], qkvw[:, k, at:at + HALF], xT[:, k, :],
                                 start=(k == 0), stop=(k == 1))
                    ins.then_inc(qk_acc, 1)
            for t in range(NT):
                for k in range(2):
                    ins = mm(bank[(7, 0)[t // 2]][:, (t % 2) * D:(t % 2 + 1) * D], xT[:, k, t * P:(t + 1) * P],
                             qkvw[:, k, 2 * D:3 * D], start=(k == 0), stop=(k == 1))
                ins.then_inc(v_acc, 1)
            pe.wait_ge(cstb_ready, 1)
            for c in range(2):
                mm(bank[1 + c][0:HALF, :], cstb[0:HALF, C_ID:C_ID + HALF],
                   cstb[0:HALF, C_CM:C_CM + T].unsqueeze(1).to_broadcast([HALF, B, T]), start=True, stop=False,
                   skip_group_check=True)
                pe.wait_ge((qx_act, qx_dve)[c], HH)
                pe.wait_ge(kT_ready, c + 1)
                for b in range(B):
                    ins = mm(bank[1 + c][0:HALF, b * T:(b + 1) * T], qx[:, c, b, :, :].rearrange("p h q -> p (h q)"),
                             kT[:, c, b * T:(b + 1) * T], start=False, stop=(b == B - 1), skip_group_check=True)
                ins.then_inc(s_acc, 1)
            for c in range(2):
                pe.wait_ge(prob_ready, c + 1)
                for t in range(NT):
                    ins = nc.tensor.transpose(bank[3 + t][:, c * HALF:(c + 1) * HALF], prob[:, c, t * P:(t + 1) * P],
                                              ident[0:HALF, 0:HALF])
                    if c == 1:
                        ins.then_inc(p_T, 1)
            pe.wait_ge(ones_ready, 1)
            pe.wait_ge(v_ready, NT)
            for t in range(NT):
                pe.wait_ge(px_ready, t + 1)
                for hd in range(HEADS):
                    ins = mm(bank[(7 + t) % 8][:, hd * (DH + 1):(hd + 1) * (DH + 1)],
                             px[:, t, hd, :, :].rearrange("p b q -> p (b q)"), v[:, t, hd, :], start=True, stop=True)
                ins.then_inc(o_acc, 1)
            for t in range(NT):
                pe.wait_ge(o_ready, t + 1)
                ins = transpose_rows(t, (bank[3], bank[4]), o)
            ins.then_inc(o_T, 1)
            pe.wait_ge(oT_act, 1)
            pe.wait_ge(oT_dve, 1)
            for t in range(NT):
                for k in range(2):
                    ins = mm(bank[(5 + t) % 8][:, 0:D], oT[:, k, t * P:(t + 1) * P], projw[:, k, :],
                             start=(k == 0), stop=(k == 1))
                ins.then_inc(x1_acc, 1)

            for t in range(NT):
                pe.wait_ge(ln_ready, 3 * NT + t + 1)
                ins = transpose_rows(t, (bank[1], bank[2]), xh)
            ins.then_inc(ln_T, 1)
            pe.wait_ge(xT_act, 3)
            pe.wait_ge(xT_dve, 3)
            for t in range(NT):
                for k in range(2):
                    ins = mm(bank[3][:, t * E:(t + 1) * E], xT[:, k, t * P:(t + 1) * P], gatew[:, k, :],
                             start=(k == 0), stop=(k == 1))
            ins.then_inc(lg_acc, 1)
            pe.wait_ge(hotb_ready, 1)
            flat = hotb[:, :, :].rearrange("p j e -> p (j e)")
            mm(bank[4][:, 0:J * E], cstb[:, C_TRI:C_TRI + P], flat, start=True, stop=False, skip_group_check=True)
            for j in range(J - 1):
                ins = mm(bank[4][:, (j + 1) * E:J * E], cstb[:, C_ONE:C_ONE + P],
                         hotb[:, j:j + 1, :].to_broadcast([P, J - 1 - j, E]), start=False, stop=(j == J - 2),
                         skip_group_check=True)
            ins.then_inc(pos_acc, 1)

            def to_channels(e):
                pe.wait_ge(slot_loaded[2 * e // E], 16)
                if e >= 2:
                    pe.wait_ge(xbT_ready, 2 * (e - 1))
                for c in range(2):
                    for m in range(2):
                        ins = nc.tensor.transpose(bank[5 + e % 2][0:HALF, c * CAP + m * M2:c * CAP + (m + 1) * M2],
                                                  slot_rows[:, 2 * e + m, c * HALF:(c + 1) * HALF], ident[0:M2, 0:M2])
                ins.then_inc(xb_T, 1)

            def hidden(e):
                pe.wait_ge(xbT_ready, 2 * (e + 1))
                pe.wait_ge(in_fc[e], 16)
                if e >= 2:
                    pe.wait_ge(hid_ready, KF * (e - 1))
                for f in range(KF):
                    to = bank[2 * (e % 2) + f // (KF // 2)][:, f % (KF // 2) * CAP:(f % (KF // 2) + 1) * CAP]
                    for c in range(2):
                        ins = mm(to, fcw[:, e, c, f * P:(f + 1) * P], xbT[:, e % 2, c, :], start=(c == 0), stop=(c == 1))
                    if f % (KF // 2) == KF // 2 - 1:
                        ins.then_inc(fc_acc, 1)

            def project(e):
                pe.wait_ge(in_pj[e], 32 if e == 0 else 16)
                pe.wait_ge(hid_ready, KF * (e + 1))
                if e >= 2:
                    pe.wait_ge(y_ready, e - 1)
                for m in range(2):
                    for f in range(KF):
                        ins = mm(bank[(4, 7)[e % 2]][0:M2, m * D:(m + 1) * D], hid[:, e % 2, f, m * M2:(m + 1) * M2],
                                 pjw[:, e, f, :], start=(f == 0), stop=(f == KF - 1))
                ins.then_inc(pj_acc, 1)

            to_channels(0)
            for e in range(E):
                if e + 1 < E:
                    to_channels(e + 1)
                hidden(e)
                if e >= 1:
                    project(e - 1)
            project(E - 1)

        @block.vector
        def _(dve):
            V = nc.vector
            steps = [0]

            def step(ins):
                steps[0] += 1
                ins.then_inc(dve_step, 1)
                dve.wait_ge(dve_step, steps[0])

            norms = [0]

            def layer_norm(src, to, signal):
                for t in range(NT):
                    ins = V.bn_stats(st[:, t, :], src[:, t, :])
                step(ins)
                for t in range(NT):
                    ins = V.bn_aggr(mv[:, t, :], st[:, t, :])
                ins.then_inc(var_ready, 1)
                norms[0] += 1
                dve.wait_ge(rstd_ready, norms[0])
                for t in range(NT):
                    V.tensor_scalar(to[:, t, :], src[:, t, :], mv[:, t, 0:1], rstd[:, t:t + 1],
                                    ALU.subtract, ALU.mult).then_inc(signal, 1)

            dve.wait_ge(in_rows, 16)
            for t in range(NT):
                dve.wait_ge(tok_acc, t + 1)
                V.tensor_tensor(h[:, t, :], bank[t][:, 0:D], row[:, 0, :], ALU.add).then_inc(h_ready, 1)
            dve.wait_ge(h_ready, NT)
            layer_norm(h, xh, ln_ready)
            dve.wait_ge(in_small, 48)
            dve.wait_ge(in_cst, 16)
            V.tensor_scalar(ndtb[:], spt[0:SS, SP_DT:SP_DT + 1], -1.0, None, ALU.mult).then_inc(small_ready, 1)
            dve.wait_ge(ln_T, 1)
            V.tensor_copy(xT[:, 1, :], bank[5][0:HALF, :]).then_inc(xT_dve, 1)
            V.tensor_scalar(qbm[:], hmask, qpt[:, QP_QB:QP_QB + 1], None, ALU.mult).then_inc(small_ready, 1)

            for m in range(KI):
                dve.wait_ge(conv_in, m + 1)
                tap = PP_CW + m * TAPS
                step(V.tensor_scalar(conv[:, 1, m, :], conv[:, 0, m, :], ppt[:, tap + TAPS - 1:tap + TAPS], None, ALU.mult))
                xv = conv[:, 0, m, :].rearrange("p (b t) -> p b t", b=B)
                sv = conv[:, 1, m, :].rearrange("p (b t) -> p b t", b=B)
                for s in range(1, TAPS):
                    ins = V.scalar_tensor_tensor(sv[:, :, s:T], xv[:, :, 0:T - s], ppt[:, tap + TAPS - 1 - s:tap + TAPS - s],
                                                 sv[:, :, s:T], ALU.mult, ALU.add)
                    if s < TAPS - 1:
                        step(ins)
                ins.then_inc(conv_out, 1)
            dve.wait_ge(xrep_ready, 1)
            dve.wait_ge(st_acc, 2)
            V.scalar_tensor_tensor(bx[:], bank[2][SS:2 * SS, :], spt[SS:2 * SS, SP_DT:SP_DT + 1], xrep[SS:2 * SS, :],
                                   ALU.add, ALU.mult)
            dve.wait_ge(decay_ready, 1)
            step(V.memset(decay[:].rearrange("p (b t) -> p b t", b=B)[:, :, 0:1], 0.0))
            step(V.tensor_tensor_scan(hs, decay[:], bx[:], 0.0, ALU.mult, ALU.add))
            dve.wait_ge(st_acc, 3)
            dve.wait_ge(sz_ready, 1)
            step(V.scalar_tensor_tensor(cz[:], bank[3][0:SS, :], spt[0:SS, SP_C:SP_C + 1], sz[:], ALU.add, ALU.mult))
            V.tensor_tensor(cz[:], hs, cz[:], ALU.mult).then_inc(g_ready, 1)
            dve.wait_ge(hb_ready, 1)
            for t in range(NT):
                dve.wait_ge(ssm_acc, t + 1)
                V.tensor_tensor(h2[:, t, :], bank[(5 + t) % 8][:, 0:D], h[:, t, :], ALU.add).then_inc(h2_ready, 1)
            dve.wait_ge(h2_ready, NT)
            layer_norm(h2, xp, ln_ready)
            dve.wait_ge(ln_ready, 2 * NT)
            layer_norm(xp, xh, ln_ready)

            dve.wait_ge(ln_T, 2)
            V.tensor_scalar(xT[:, 1, :], bank[2][0:HALF, :], qpt[:, QP_L1W + 1:QP_L1W + 2], qpt[:, QP_L1B + 1:QP_L1B + 2],
                            ALU.mult, ALU.add).then_inc(xT_dve, 1)
            dve.wait_ge(qk_acc, 2)
            for hd in range(HH):
                V.tensor_scalar(qx[:, 1, :, hd, :], bank[4][0:HALF, :].rearrange("p (b q) -> p b q", b=B),
                                qpt[:, QP_QB + 1:QP_QB + 2], hmask[:, hd:hd + 1], ALU.add, ALU.mult).then_inc(qx_dve, 1)
            for t in range(NT):
                dve.wait_ge(v_acc, 2 * (t // 2) + 2)
                V.tensor_tensor(v[:, t, :, 0:DH], bank[(7, 0)[t // 2]][:, (t % 2) * D:(t % 2 + 1) * D].rearrange(
                    "p (h d) -> p h d", h=HEADS), row[:, 2, :].rearrange("p (h d) -> p h d", h=HEADS),
                    ALU.add).then_inc(v_ready, 1)
            for c in range(2):
                dve.wait_ge(s_acc, c + 1)
                scores = bank[1 + c][0:HALF, :].rearrange("p (b k) -> p b k", b=B)
                step(V.tensor_reduce(nmax[:, c, :], scores, AX_X, ALU.max))
                V.tensor_tensor(prob[:, c, :].rearrange("p (b k) -> p b k", b=B), scores,
                                nmax[:, c, :].unsqueeze(2).to_broadcast([HALF, B, T]), ALU.subtract).then_inc(shifted, 1)
            for t in range(NT):
                dve.wait_ge(p_T, t + 1)
                V.tensor_tensor(px[:, t, :, :, :],
                                bank[3 + t][:, 0:D].rearrange("p (h q) -> p h q", h=HEADS).unsqueeze(2).to_broadcast(
                                    [P, HEADS, BT, T]),
                                bmask.unsqueeze(1).unsqueeze(3).to_broadcast([P, HEADS, BT, T]),
                                ALU.mult).then_inc(px_ready, 1)
            for t in range(NT):
                dve.wait_ge(o_acc, t + 1)
                ot = bank[(7 + t) % 8][:, 0:HEADS * (DH + 1)].rearrange("p (h d) -> p h d", h=HEADS)
                step(V.reciprocal(den[:, t, :], ot[:, :, DH]))
                V.tensor_tensor(o[:, t, :].rearrange("p (h d) -> p h d", h=HEADS), ot[:, :, 0:DH],
                                den[:, t, :].unsqueeze(2).to_broadcast([P, HEADS, DH]), ALU.mult).then_inc(o_ready, 1)
            dve.wait_ge(o_T, 1)
            V.tensor_copy(oT[:, 1, :], bank[4][0:HALF, :]).then_inc(oT_dve, 1)
            dve.wait_ge(xpb_ready, 1)
            for t in range(NT):
                dve.wait_ge(x1_acc, t + 1)
                ins = V.tensor_tensor(x1[:, t, :], bank[(5 + t) % 8][:, 0:D], xp[:, t, :], ALU.add)
            step(ins)
            layer_norm(x1, xh, ln_ready)

            dve.wait_ge(ln_T, 3)
            V.tensor_scalar(xT[:, 1, :], bank[2][0:HALF, :], qpt[:, QP_L2W + 1:QP_L2W + 2], qpt[:, QP_L2B + 1:QP_L2B + 2],
                            ALU.mult, ALU.add).then_inc(xT_dve, 1)
            dve.wait_ge(lg_acc, 1)
            step(V.tensor_copy(lg[:], bank[3][:, 0:NT * E].rearrange("p (t e) -> p t e", t=NT)))
            rev = cst[:, C_REV:C_REV + NT * E].rearrange("p (t e) -> p t e", t=NT)
            for k, src in enumerate((lg, lg2)):
                c = slice(k * NT, (k + 1) * NT)
                step(V.tensor_reduce(top[:, c], src[:], AX_X, ALU.max))
                step(V.tensor_tensor(cand[:], src[:], top[:, c].unsqueeze(2).to_broadcast([P, NT, E]), ALU.is_equal))
                step(V.tensor_tensor(cand[:], cand[:], rev, ALU.mult))
                step(V.tensor_reduce(first[:, c], cand[:], AX_X, ALU.max))
                step(V.tensor_tensor(hot[:, c, :], rev, first[:, c].unsqueeze(2).to_broadcast([P, NT, E]), ALU.is_equal))
                if k == 0:
                    step(V.scalar_tensor_tensor(lg2[:], hot[:, c, :], -3.0e38, lg[:], ALU.mult, ALU.add))
            V.tensor_copy(hotb[:], hot[:]).then_inc(hotb_ready, 1)
            V.tensor_tensor(gap[:], top[:, NT:J], top[:, 0:NT], ALU.subtract).then_inc(gap_ready, 1)
            e160 = cst[:, C_E160:C_E160 + J * E].rearrange("p (j e) -> p j e", j=J)
            step(V.tensor_tensor(off[:], hot[:], e160, ALU.mult))
            V.tensor_reduce(offs[:], off[:], AX_X, ALU.add)
            dve.wait_ge(pos_acc, 1)
            step(V.tensor_tensor(pos[:], bank[4][:, 0:J * E].rearrange("p (j e) -> p j e", j=J), hot[:], ALU.mult))
            step(V.tensor_reduce(rank[:], pos[:], AX_X, ALU.add))
            V.tensor_scalar(kept[:], rank[:], float(CAP), None, ALU.is_lt)
            step(V.tensor_tensor(slot[:], rank[:], offs[:], ALU.add))
            trash = cst[:, C_TRASH:C_TRASH + J]
            step(V.tensor_tensor(dst[:], slot[:], trash, ALU.subtract))
            step(V.tensor_tensor(dst[:], dst[:], kept[:], ALU.mult))
            V.tensor_tensor(put[:], dst[:], trash, ALU.add).then_inc(put_ready, 1)
            V.tensor_tensor(get[:], slot[:], kept[:], ALU.mult).then_inc(get_ready, 1)
            dve.wait_ge(wgt_ready, 2)
            step(V.tensor_tensor(wgt[:], wgt[:], kept[:], ALU.mult))

            def affine(e):
                dve.wait_ge(xb_T, e + 1)
                if e >= 2:
                    dve.wait_ge(fc_acc, 2 * (e - 1))
                for c in range(2):
                    V.tensor_scalar(xbT[:, e % 2, c, :], bank[5 + e % 2][0:HALF, c * CAP:(c + 1) * CAP],
                                    qpt[:, QP_L2W + c:QP_L2W + c + 1], qpt[:, QP_L2B + c:QP_L2B + c + 1],
                                    ALU.mult, ALU.add).then_inc(xbT_ready, 1)

            def outputs(e):
                dve.wait_ge(pj_acc, e + 1)
                V.tensor_tensor(y_rows[:, 2 * e:2 * e + 2, :],
                                bank[(4, 7)[e % 2]][0:M2, 0:2 * D].rearrange("p (n d) -> p n d", n=2),
                                pjb[:, e:e + 1, :].to_broadcast([M2, 2, D]), ALU.add).then_inc(y_ready, 1)

            affine(0)
            affine(1)
            for e in range(E):
                if e + 2 < E:
                    affine(e + 2)
                outputs(e)
            dve.wait_ge(base_ready, 1)
            for t in range(NT):
                dve.wait_ge(gathered[t], 16 * TOPK)
                step(V.scalar_tensor_tensor(h2[:, t, :], got[:, t, :], wgt[:, t:t + 1], h2[:, t, :], ALU.mult, ALU.add))
                V.scalar_tensor_tensor(h2[:, t, :], got[:, NT + t, :], wgt[:, NT + t:NT + t + 1], h2[:, t, :],
                                       ALU.mult, ALU.add).then_inc(res_ready, 1)


def kernel(x, L0_tok_W, L0_tok_b, L0_attn_W_in, L0_attn_b_in, L0_attn_conv_w, L0_attn_conv_b, L0_attn_W_x,
           L0_attn_b_x, L0_attn_W_dt, L0_attn_b_dt, L0_attn_W_out, L0_attn_b_out, L0_ffn_ln1_w, L0_ffn_ln1_b,
           L0_ffn_ln2_w, L0_ffn_ln2_b, L0_ffn_attn_qkv_w, L0_ffn_attn_qkv_b, L0_ffn_attn_proj_w,
           L0_ffn_attn_proj_b, L0_ffn_w_g, L0_ffn_exp_fc_w, L0_ffn_exp_fc_b, L0_ffn_exp_proj_w,
           L0_ffn_exp_proj_b):
    import concourse.bacc as bacc
    from concourse.bass_utils import run_bass_kernel_spmd

    def a(v):
        return np.asarray(v)

    def halves(w):
        return a(w).reshape(2, HALF, -1).transpose(1, 0, 2)

    def chunks(w):
        w = a(w)
        return w.reshape(w.shape[0] // P, P, -1).transpose(1, 0, 2)

    def by_j(w):
        return np.tile(w, S)

    def by_i(w):
        return np.repeat(w, S, axis=-1)

    side = x.shape[-1] // 4
    patches = a(x).reshape(B, 3, 4, side, 4, side).transpose(3, 5, 1, 0, 2, 4).reshape(PIX, N)
    b_dt, b_x, b_in = a(L0_attn_b_dt), a(L0_attn_b_x), a(L0_attn_b_in)
    w_x, qkv_b = a(L0_attn_W_x), a(L0_ffn_attn_qkv_b)
    pp = np.concatenate([
        b_in[:INNER].reshape(KI, P).T,
        a(L0_attn_conv_w).reshape(KI, P, TAPS).transpose(1, 0, 2).reshape(P, KI * TAPS),
        a(L0_attn_conv_b).reshape(KI, P).T,
        a(L0_ffn_exp_fc_b).reshape(E, KF, P).transpose(2, 0, 1).reshape(P, E * KF)], axis=1)
    qp = np.concatenate([a(v).reshape(2, HALF).T for v in (
        L0_ffn_ln1_w, L0_ffn_ln1_b, L0_ffn_ln2_w, L0_ffn_ln2_b, qkv_b[:D], qkv_b[D:2 * D])], axis=1)
    state_b = np.stack([
        np.concatenate([by_j(b_dt[:S]), by_j(b_x[2 * S:3 * S])]),
        np.concatenate([by_j(b_x[3 * S:4 * S])] * 2),
        np.concatenate([by_i(b_in[INNER:WIN])] * 2)], axis=1)
    data = {
        "patches": patches.reshape(KP, P, N).transpose(1, 0, 2),
        "tok_w": chunks(a(L0_tok_W).T),
        "w_in": halves(a(L0_attn_W_in)[:, :INNER]),
        "w_z": halves(by_i(a(L0_attn_W_in)[:, INNER:WIN])),
        "w_state": chunks(np.concatenate([by_j(a(L0_attn_W_dt)[:, :S]), by_j(w_x[:, 2 * S:3 * S]),
                                          by_j(w_x[:, 3 * S:4 * S])], axis=1)),
        "w_out": np.repeat(a(L0_attn_W_out)[:S], S, axis=0),
        "qkv_w": halves(L0_ffn_attn_qkv_w),
        "proj_w": halves(L0_ffn_attn_proj_w),
        "gate_w": halves(L0_ffn_w_g),
        "fc_w": a(L0_ffn_exp_fc_w).reshape(E, 2, HALF, F).transpose(2, 0, 1, 3),
        "pj_w": a(L0_ffn_exp_proj_w).reshape(E, KF, P, D).transpose(2, 0, 1, 3),
        "pp": pp,
        "qp": qp,
        "sp_par": state_b,
        "rows": np.stack([a(L0_tok_b), a(L0_attn_b_out), qkv_b[2 * D:], a(L0_ffn_attn_proj_b)]),
        "pj_b": a(L0_ffn_exp_proj_b).reshape(E, D),
        "consts": constants(),
    }
    nc = bacc.Bacc("TRN2", target_bir_lowering=False, num_devices=1)
    arrays, args = {}, []
    for name, v in data.items():
        v = np.ascontiguousarray(v)
        arrays[f"in_{name}"] = v
        args.append(nc.dram_tensor(f"in_{name}", v.shape, mybir.dt.from_np(v.dtype), kind="ExternalInput").ap())
    args.append(nc.dram_tensor("out_0_dram", (N, D), F32, kind="ExternalOutput").ap())
    vit_block(nc, *args)
    r = run_bass_kernel_spmd(nc, [arrays], core_ids=[0])
    return r.results[0]["out_0_dram"].reshape(B, T, D)
```

```python
from contextlib import ExitStack

import numpy as np

import concourse.bass as bass
from concourse import mybir
from concourse.alu_op_type import AluOpType as ALU

F32 = mybir.dt.float32
BF16 = mybir.dt.bfloat16
I32 = mybir.dt.int32
ACT = mybir.ActivationFunctionType
AX_X = mybir.AxisListType.X

P = 128
B, T = 32, 16
N = B * T
NT = N // P
BT = P // T
D = 192
HALF = D // 2
PIX = 768
KP = PIX // P
PIECES = 6
INNER = 384
KI = INNER // P
S = 8
SS = S * S
TAPS = 4
HEADS, DH = 12, 16
HH = HEADS // 2
PAIR = 2 * DH
PAIRS = HALF // PAIR
E, TOPK = 8, 2
CAP = 160
CAP += CAP % 2
assert CAP == int(TOPK * 1.25 * N / E)
M2 = CAP // 2
QUAD = 4
REST = CAP - P
assert REST * QUAD == P
HB = 5
F = 768
KF = F // P
J = TOPK * NT
EPS = 1e-5
NEG = -1.0e30
ZERO = 256
WIN = INNER + S

PP_BIN, PP_CW, PP_CB, PP_FCB = 0, KI, KI + KI * TAPS, 2 * KI + KI * TAPS
PP_W = PP_FCB + E * KF
QP_L1W, QP_L1B, QP_L2W, QP_L2B, QP_QB, QP_KB, QP_W = 0, 2, 4, 6, 8, 10, 12
SP_DT, SP_C, SP_Z, SP_W = 0, 1, 2, 3
C_ID, C_TRI, C_ONE = 0, P, 2 * P
C_CM = 3 * P
C_TOKEN = C_CM + T
C_SLOT = C_TOKEN + NT * E * 3
C_BF = C_SLOT + CAP
C_HM = C_BF
C_BM = C_HM + 2
C_CHOICE = C_BM + 2
C_SEL = C_CHOICE + J * E
C_HALF = C_SEL + P
C_HOLE = C_HALF + 2 * NT
C_NHOLE = C_HOLE + E + E // QUAD
C_W = C_NHOLE + E + E // QUAD
PARTS = 3
NOWHERE = 1000.0

OUTPUTS = []
for e in range(E):
    OUTPUTS.append((e, e))
    if e % QUAD == QUAD - 1:
        OUTPUTS.append((e - QUAD + 1, e))


WARM = (6, 24, 4, 8, 6, 20, 4, 12, 6)


def constants():
    c = np.zeros((P, C_W), np.float32)
    p = np.arange(P)
    c[:, C_ID:C_ID + P] = np.eye(P)
    c[:, C_TRI:C_TRI + P] = p[:, None] < p[None, :]
    c[:, C_ONE:C_ONE + P] = 1.0
    c[:HALF, C_CM:C_CM + T] = np.where(np.arange(T)[None, :] <= (p[:HALF] % T)[:, None], 0.0, NEG)
    c[:, C_BM:C_BM + 2] = p[:, None] // T % 2 == np.arange(2)[None, :]
    c[:, C_HM:C_HM + 2] = c[:, C_BM:C_BM + 2] * DH ** -0.5
    token = c[:, C_TOKEN:C_TOKEN + NT * E * 3].reshape(P, NT, E, 3)
    token[..., 0] = p[:, None, None]
    token[..., 1] = 1.0
    token[..., 2] = np.arange(NT)[None, :, None] * P
    c[:, C_TOKEN:C_TOKEN + NT * E * 3] = token.reshape(P, -1)
    c[:, C_SLOT:C_SLOT + CAP] = np.arange(CAP)
    c[:, C_CHOICE:C_CHOICE + J * E] = np.tile(np.arange(E), J)
    hole = J * P + np.arange(len(OUTPUTS))[None, :] * P + p[:, None]
    c[:, C_HOLE:C_HOLE + len(OUTPUTS)] = hole
    c[:, C_NHOLE:C_NHOLE + len(OUTPUTS)] = -hole
    c[:S, C_SEL + SS:C_SEL + 2 * SS] = np.arange(SS)[None, :] // S == np.arange(S)[:, None]
    c[:, C_HALF:C_HALF + 2 * NT] = -0.5
    return c


def vit_block(nc, patches, tok_w, w_in, w_z, w_state, w_out, qkv_w, proj_w, gate_w, fc_w, pj_w,
              pp, qp, sp_par, rows, pj_b, consts, out):
    ctx = ExitStack()
    with ctx:
        def sb(name, shape, dt=F32):
            return ctx.enter_context(nc.sbuf_tensor(name, shape, dt))

        def sem(name):
            return ctx.enter_context(nc.semaphore(name))

        choice_out = nc.dram_tensor("choice_out", (J * P + len(OUTPUTS) * P, D), F32).ap()

        bank = [ctx.enter_context(nc.psum_tensor(f"bank{i}", [P, 512], F32)) for i in range(8)]

        cst = sb("cst", [P, C_W])
        cstb = sb("cstb", [P, C_BF], BF16)
        ppt = sb("ppt", [P, PP_W])
        qpt = sb("qpt", [HALF, QP_W])
        spt = sb("spt", [P, SP_W])
        row = sb("row", [P, 4, D])
        pjb = sb("pjb", [P, E + E // QUAD, D])
        pat = sb("pat", [P, KP, N])
        tokw = sb("tokw", [P, KP, D])
        win = sb("win", [HALF, 2, INNER])
        winz = sb("winz", [HALF, 2, SS])
        wst = sb("wst", [P, KI, 3 * SS])
        wout = sb("wout", [SS, D])
        qkvw = sb("qkvw", [HALF, 2, 3 * D])
        projw = sb("projw", [HALF, 2, D])
        gatew = sb("gatew", [HALF, 2, E])
        fcw = sb("fcw", [HALF, E, 2, F])
        pjw = sb("pjw", [P, E, KF, D])
        zeros = sb("zeros", [P, ZERO])

        h = sb("h", [P, NT, D])
        h2 = sb("h2", [P, NT, D])
        xh = sb("xh", [P, NT, D])
        xp = sb("xp", [P, NT, D])
        x1 = sb("x1", [P, NT, D])
        st = sb("st", [P, NT, 6])
        mv = sb("mv", [P, NT, 2])
        ve = sb("ve", [P, 2 * NT])
        rstd = sb("rstd", [P, 2 * NT])
        xT = sb("xT", [HALF, 2, N])
        conv = sb("conv", [P, 2, KI, N])
        xc = sb("xc", [P, KI, N])
        ndtb = sb("ndtb", [SS, 1])
        sz = sb("sz", [SS, N])
        xrep = sb("xrep", [P, N])
        decay = sb("decay", [SS, N])
        bx = sb("bx", [SS, N])
        cz = sb("cz", [SS, N])
        hs = conv[0:SS, 0, 0, :]
        qbm = sb("qbm", [HALF, 2])
        kT = sb("kT", [HALF, 2, N])
        hid = sb("hid", [P, HB, KF, CAP])
        flat_hid = hid[:, :, :, :].rearrange("p b f s -> p (b f s)")
        qx = flat_hid[0:HALF, 0:4 * N].rearrange("p (c b a q) -> p c b a q", c=2, b=B, a=2)
        px = flat_hid[:, 4 * N:4 * N + NT * HEADS * 2 * T].rearrange("p (t h a q) -> p t h a q", t=NT, h=HEADS, a=2)
        v = sb("v", [P, NT, HEADS, DH + 1])
        nmax = sb("nmax", [HALF, 2, B])
        prob = xc[0:HALF, 0:2, :]
        den = sb("den", [P, NT, HEADS])
        o = tokw[:, 0:NT, :]
        oT = kT
        top = sb("top", [P, NT, 8])
        chosen = sb("chosen", [P, NT, 8], mybir.dt.uint32)
        hotb = sb("hotb", [P, J, E], BF16)
        gap = sb("gap", [P, NT])
        wgt = sb("wgt", [P, J])
        pos = sb("pos", [P, J, E])
        miss = sb("miss", [P, NT, E])
        place = sb("place", [P, NT, E])
        oh = sb("oh", [P, 2, NT, CAP], BF16)
        row_of = sb("row_of", [P, len(OUTPUTS), 4])
        put = sb("put", [P, len(OUTPUTS)], I32)
        bcw = sb("bcw", [P, KI])
        got = pat[:, 0:3, :].rearrange("p a b -> p (a b)").rearrange("p (j d) -> p j d", j=J)
        left = tokw[:, 0:NT, :]
        parts = pat[:, 3:KP, :].rearrange("p a b -> p (a b)").bitcast(BF16)[:, 0:PARTS * NT * D].rearrange(
            "p (n t d) -> p n t d", n=PARTS, t=NT)

        flat_conv = conv[:, :, :, :].rearrange("p x a b -> p (x a b)")
        xbT = flat_conv[0:HALF, len(OUTPUTS) * D:len(OUTPUTS) * D + 4 * CAP].rearrange("p (b c s) -> p b c s", b=2, c=2)
        y_rows = conv[:, :, :, :].rearrange("p x a b -> p (x a b)")[:, 0:len(OUTPUTS) * D].rearrange(
            "p (n d) -> p n d", d=D)
        token = cstb[:, C_TOKEN:C_TOKEN + NT * E * 3].rearrange("p (t e n) -> p t e n", t=NT, e=E)
        zeros_b = zeros[:].bitcast(BF16)
        ident = cst[:, C_ID:C_ID + P]
        hmask = cst[0:HALF, C_HM:C_HM + 2]
        bmask = cst[:, C_BM:C_BM + 2]

        in_tok = [sem(f"in_tok{i}") for i in range(PIECES)]
        in_cst, in_small, in_ssm, in_rows, in_attn, in_zero = (sem(n) for n in (
            "in_cst", "in_small", "in_ssm", "in_rows", "in_attn", "in_zero"))
        in_fc = [sem(f"in_fc{e}") for e in range(E)]
        in_pj = [sem(f"in_pj{e}") for e in range(E)]
        in_pjb = sem("in_pjb")
        zeros_ready, zero_rows = sem("zeros_ready"), sem("zero_rows")
        cstb_ready = sem("cstb_ready")
        tok_acc, ln_T, xz_acc, st_acc, ssm_acc, qk_acc, v_acc, s_acc, p_T, o_acc, o_T, x1_acc = (sem(n) for n in (
            "tok_acc", "ln_T", "xz_acc", "st_acc", "ssm_acc", "qk_acc", "v_acc", "s_acc", "p_T", "o_acc", "o_T",
            "x1_acc"))
        lg_acc, pos_acc, xb_acc, fc_acc, pj_acc = (sem(n) for n in ("lg_acc", "pos_acc", "xb_acc", "fc_acc", "pj_acc"))
        ln_ready, xT_act, xT_dve, conv_in, conv_out, xc_ready, small_ready = (sem(n) for n in (
            "ln_ready", "xT_act", "xT_dve", "conv_in", "conv_out", "xc_ready", "small_ready"))
        sz_ready, xrep_ready, decay_ready, g_ready, hb_ready, h_ready = (sem(n) for n in (
            "sz_ready", "xrep_ready", "decay_ready", "g_ready", "hb_ready", "h_ready"))
        qx_act, qx_dve, kT_ready, v_ready, shifted, prob_ready, px_ready, o_ready, oT_act, oT_dve = (
            sem(n) for n in ("qx_act", "qx_dve", "kT_ready", "v_ready", "shifted", "prob_ready", "px_ready",
                             "o_ready", "oT_act", "oT_dve"))
        xpb_ready, h2_ready, base_ready, gap_ready, wgt_ready, hotb_ready, put_ready, oh_ready = (sem(n) for n in (
            "xpb_ready", "h2_ready", "base_ready", "gap_ready", "wgt_ready", "hotb_ready", "put_ready",
            "oh_ready"))
        part_act, part_pool, bcw_ready, token_ready = (sem(n) for n in ("part_act", "part_pool", "bcw_ready", "token_ready"))
        scattered, xbT_ready, hid_ready, y_ready, res_ready, stored = (
            sem(n) for n in ("scattered", "xbT_ready", "hid_ready", "y_ready", "res_ready", "stored"))
        gathered = [sem(f"gathered{t}") for t in range(NT)]
        dve_step, pool_step = sem("dve_step"), sem("pool_step")
        ln_pool, x1_ready, put_sum = sem("ln_pool"), sem("x1_ready"), sem("put_sum")
        ones_ready, var_ready, rstd_ready = sem("ones_ready"), sem("var_ready"), sem("rstd_ready")

        block = ctx.enter_context(nc.Block())

        @block.sync
        def _(sync):
            for i in range(PIECES):
                k = slice(i * KP // PIECES, (i + 1) * KP // PIECES)
                sync.dma_start(pat[:, k, :], patches[:, k, :]).then_inc(in_tok[i], 16)
            sync.dma_start(win[:], w_in).then_inc(in_ssm, 16)
            sync.dma_start(winz[:], w_z).then_inc(in_ssm, 16)
            sync.dma_start(wst[:], w_state).then_inc(in_ssm, 16)
            sync.dma_start(wout[:], w_out).then_inc(in_ssm, 16)
            sync.dma_start(qkvw[:], qkv_w).then_inc(in_attn, 16)
            sync.dma_start(projw[:], proj_w).then_inc(in_attn, 16)
            sync.dma_start(gatew[:], gate_w).then_inc(in_attn, 16)
            sync.wait_ge(zeros_ready, 1)
            sync.dma_start(choice_out[0:J * P, :].rearrange("(p n) d -> p (n d)", p=P).rearrange(
                "p (r z) -> p r z", z=ZERO), zeros[:].unsqueeze(1).to_broadcast([P, J * D // ZERO, ZERO])).then_inc(
                    zero_rows, 16)
            for e in range(E):
                sync.dma_start(fcw[:, e, :, :], fc_w[:, e, :, :]).then_inc(in_fc[e], 16)
                sync.dma_start(pjw[:, e, :, :], pj_w[:, e, :, :]).then_inc(in_pj[e], 16)
            sync.wait_ge(scattered, 16 * len(OUTPUTS))
            for t in range(NT):
                sync.dma_start(got[:, t:J:NT, :], choice_out[0:J * P, :].rearrange("(j p) d -> p j d", p=P)[
                    :, t:J:NT, :]).then_inc(gathered[t], 16)
            for t in range(NT):
                sync.wait_ge(res_ready, t + 1)
                sync.dma_start(out[t * P:(t + 1) * P, :], h2[:, t, :]).then_inc(stored, 16)
            sync.wait_ge(stored, 16 * NT)

        @block.gpsimd
        def _(pool):
            steps = [0]

            def step(ins):
                steps[0] += 1
                ins.then_inc(pool_step, 1)
                pool.wait_ge(pool_step, steps[0])

            nc.gpsimd.memset(zeros[:], 0.0).then_inc(zeros_ready, 1)
            nc.gpsimd.memset(v[:, :, :, DH:DH + 1], 1.0).then_inc(ones_ready, 1)

            def rstd_of(n, width):
                pool.wait_ge(var_ready, n)
                nc.gpsimd.tensor_tensor(rstd[:, 0:width], ve[:, 0:width], cst[:, C_HALF:C_HALF + width],
                                        ALU.pow).then_inc(rstd_ready, 1)

            def rows_of_last_tile(src, to, factor):
                nc.gpsimd.tensor_scalar(to[:, NT - 1, :], src[:, NT - 1, :], mv[:, NT - 1, 0:1],
                                        rstd[:, factor * NT + NT - 1:factor * NT + NT], ALU.subtract,
                                        ALU.mult).then_inc(ln_pool, 1)

            pool.wait_ge(in_cst, 16)
            rstd_of(1, NT)
            pool.wait_ge(rstd_ready, 1)
            rows_of_last_tile(h, xh, 0)
            pool.wait_ge(in_rows, 16)
            pool.wait_ge(ln_ready, NT - 1)
            pool.wait_ge(ln_pool, 1)
            nc.gpsimd.tensor_tensor(h[:], h[:], row[:, 1:2, :].to_broadcast([P, NT, D]), ALU.add).then_inc(hb_ready, 1)
            rstd_of(2, 2 * NT)
            pool.wait_ge(rstd_ready, 2)
            rows_of_last_tile(h2, xh, 0)
            for t in range(NT):
                ins = nc.gpsimd.tensor_scalar(xp[:, t, :], h2[:, t, :], mv[:, t, 0:1], rstd[:, NT + t:NT + t + 1],
                                              ALU.subtract, ALU.mult)
            step(ins)
            nc.gpsimd.tensor_tensor(xp[:], xp[:], row[:, 3:4, :].to_broadcast([P, NT, D]), ALU.add).then_inc(xpb_ready, 1)
            rstd_of(3, NT)
            pool.wait_ge(rstd_ready, 3)
            rows_of_last_tile(x1, xh, 0)
            pool.wait_ge(part_act, 1)
            nc.gpsimd.tensor_tensor(left, xh[:], parts[:, 0, :, :], ALU.subtract).then_inc(part_pool, 1)
            pool.wait_ge(part_act, 2)
            pool.wait_ge(part_pool, 1)
            nc.gpsimd.tensor_tensor(parts[:, 2, :, :], left, parts[:, 1, :, :], ALU.subtract).then_inc(part_pool, 1)
            nc.gpsimd.tensor_tensor(h2[:], h2[:], x1[:], ALU.add).then_inc(base_ready, 1)
            pool.wait_ge(zero_rows, 16)
            for n in range(len(OUTPUTS)):
                pool.wait_ge(put_ready, n + 1)
                pool.wait_ge(y_ready, n + 1)
                nc.gpsimd.indirect_dma_start(
                    out=choice_out, out_offset=bass.IndirectOffsetOnAxis(ap=put[:, n:n + 1], axis=0),
                    in_=y_rows[:, n, :], in_offset=None).then_inc(scattered, 16)

        @block.scalar
        def _(act):
            for i in range(PIECES):
                k = slice(i * KP // PIECES, (i + 1) * KP // PIECES)
                act.dma_start(tokw[:, k, :], tok_w[:, k, :]).then_inc(in_tok[i], 16)
            act.dma_start(cst[:], consts).then_inc(in_cst, 16)
            act.dma_start(ppt[:], pp).then_inc(in_small, 16)
            act.dma_start(qpt[:], qp).then_inc(in_small, 16)
            act.dma_start(spt[:], sp_par).then_inc(in_small, 16)
            act.dma_start(row[:], rows.partition_broadcast(P)).then_inc(in_rows, 16)
            act.dma_start(pjb[:, 0:E, :], pj_b.partition_broadcast(P)).then_inc(in_pjb, 16)
            for e in range(E):
                j = e % QUAD
                act.dma_start(pjb[j * REST:(j + 1) * REST, E + e // QUAD, :],
                              pj_b[e, :].partition_broadcast(REST)).then_inc(in_pjb, 16)
            act.wait_ge(in_cst, 16)
            nc.scalar.activation(cstb[:], cst[:, 0:C_BF], ACT.Copy).then_inc(cstb_ready, 1)

            act.wait_ge(ln_T, 1)
            nc.scalar.activation(xT[:, 0, :], bank[4][0:HALF, :], ACT.Copy).then_inc(xT_act, 1)
            act.wait_ge(bcw_ready, 1)
            for m in range(KI):
                act.wait_ge(xz_acc, m + 1)
                nc.scalar.activation(conv[:, 0, m, :], bank[(6 + m) % 8][:], ACT.Identity,
                                     bias=ppt[:, PP_BIN + m:PP_BIN + m + 1]).then_inc(conv_in, 1)
                own = PP_CW + m * TAPS + TAPS - 1
                nc.scalar.activation(conv[:, 1, m, :], bank[(6 + m) % 8][:], ACT.Identity, scale=ppt[:, own:own + 1],
                                     bias=bcw[:, m:m + 1]).then_inc(conv_in, 1)
            act.wait_ge(xz_acc, KI + 1)
            nc.scalar.activation(sz[:], bank[1][0:SS, :], ACT.Silu, bias=spt[0:SS, SP_Z:SP_Z + 1]).then_inc(sz_ready, 1)
            for m in range(KI):
                act.wait_ge(conv_out, m + 1)
                nc.scalar.activation(xc[:, m, :], conv[:, 1, m, :], ACT.Silu,
                                     bias=ppt[:, PP_CB + m:PP_CB + m + 1]).then_inc(xc_ready, 1)
            act.wait_ge(st_acc, 1)
            nc.scalar.activation(xrep[SS:2 * SS, :], bank[4][SS:2 * SS, :], ACT.Copy).then_inc(xrep_ready, 1)
            act.wait_ge(st_acc, 2)
            act.wait_ge(small_ready, 2)
            nc.scalar.activation(decay[:], bank[2][0:SS, :], ACT.Sigmoid, scale=-1.0, bias=ndtb[:]).then_inc(decay_ready, 1)

            act.wait_ge(ln_T, 3)
            nc.scalar.activation(xT[:, 0, :], bank[1][0:HALF, :], ACT.Identity, scale=qpt[:, QP_L1W:QP_L1W + 1],
                                 bias=qpt[:, QP_L1B:QP_L1B + 1]).then_inc(xT_act, 1)
            act.wait_ge(qk_acc, 1)
            act.wait_ge(small_ready, 2)
            for a in range(2):
                nc.scalar.activation(qx[:, 0, :, a, :], bank[3][0:HALF, :].rearrange("p (b q) -> p b q", b=B),
                                     ACT.Identity, scale=hmask[:, a:a + 1], bias=qbm[:, a:a + 1]).then_inc(qx_act, 1)
            for c in range(2):
                act.wait_ge(qk_acc, c + 3)
                nc.scalar.activation(kT[:, c, :], bank[5 + c][0:HALF, :], ACT.Identity,
                                     bias=qpt[:, QP_KB + c:QP_KB + c + 1]).then_inc(kT_ready, 1)
            for c in range(2):
                act.wait_ge(shifted, c + 1)
                nc.scalar.activation(prob[:, c, :], prob[:, c, :], ACT.Exp).then_inc(prob_ready, 1)
            act.wait_ge(o_T, 1)
            nc.scalar.activation(oT[:, 0, :], bank[3][0:HALF, :], ACT.Copy).then_inc(oT_act, 1)

            act.wait_ge(ln_T, 5)
            nc.scalar.activation(xT[:, 0, :], bank[1][0:HALF, :], ACT.Identity, scale=qpt[:, QP_L2W:QP_L2W + 1],
                                 bias=qpt[:, QP_L2B:QP_L2B + 1]).then_inc(xT_act, 1)
            act.wait_ge(ln_ready, 3 * (NT - 1))
            act.wait_ge(ln_pool, 3)
            nc.scalar.activation(parts[:, 0, :, :], xh[:], ACT.Copy).then_inc(part_act, 1)
            act.wait_ge(part_pool, 1)
            nc.scalar.activation(parts[:, 1, :, :], left, ACT.Copy).then_inc(part_act, 1)
            act.wait_ge(gap_ready, 1)
            for k in range(TOPK):
                nc.scalar.activation(wgt[:, k * NT:(k + 1) * NT], gap[:], ACT.Sigmoid,
                                     scale=(1.0, -1.0)[k]).then_inc(wgt_ready, 1)
            for e in range(E):
                for m in range(2):
                    act.wait_ge(fc_acc, 2 * e + m + 1)
                    if e >= HB:
                        act.wait_ge(pj_acc, QUAD + 1)
                    if e - HB >= QUAD:
                        act.wait_ge(pj_acc, len(OUTPUTS))
                    for n in range(KF // 2):
                        f = m * KF // 2 + n
                        nc.scalar.activation(
                            hid[:, e % HB, f, :], bank[2 * (e % 2) + m][:, n * CAP:(n + 1) * CAP], ACT.Gelu,
                            bias=ppt[:, PP_FCB + e * KF + f:PP_FCB + e * KF + f + 1]).then_inc(hid_ready, 1)

        @block.tensor
        def _(pe):
            mm = nc.tensor.matmul

            def keep_warm(to, n):
                for _ in range(n):
                    mm(to[:], zeros_b[:, 0:P], zeros_b[:], start=True, stop=True)

            def transpose_halves(to, src, signal, ready):
                for c in range(2):
                    for t in range(NT):
                        if c == 0:
                            ready(t)
                        ins = nc.tensor.transpose(to[c][0:HALF, t * P:(t + 1) * P], src[:, t, c * HALF:(c + 1) * HALF],
                                                  ident)
                    ins.then_inc(signal, 1)

            def normalised(n):
                def ready(t):
                    if t < NT - 1:
                        pe.wait_ge(ln_ready, n * (NT - 1) + t + 1)
                    else:
                        pe.wait_ge(ln_pool, n + 1)
                return ready

            pe.wait_ge(zeros_ready, 1)
            keep_warm(bank[7], WARM[0])
            for i in range(PIECES - 2):
                pe.wait_ge(in_tok[i], 32)
                for t in range(NT):
                    mm(bank[t][:, 0:D], pat[:, i, t * P:(t + 1) * P], tokw[:, i, :], start=(i == 0), stop=False)
            pe.wait_ge(in_tok[PIECES - 2], 32)
            pe.wait_ge(in_tok[PIECES - 1], 32)
            for t in range(NT):
                for i in (PIECES - 2, PIECES - 1):
                    ins = mm(bank[t][:, 0:D], pat[:, i, t * P:(t + 1) * P], tokw[:, i, :],
                             start=False, stop=(i == PIECES - 1))
                ins.then_inc(tok_acc, 1)
            pe.wait_ge(in_cst, 16)
            keep_warm(bank[7], WARM[1])
            transpose_halves((bank[4], bank[5]), xh, ln_T, normalised(0))

            pe.wait_ge(in_ssm, 64)
            keep_warm(bank[3], WARM[2])
            pe.wait_ge(xT_act, 1)
            pe.wait_ge(xT_dve, 1)
            for m in range(KI):
                for c in range(2):
                    ins = mm(bank[(6 + m) % 8][:], win[:, c, m * P:(m + 1) * P], xT[:, c, :], start=(c == 0), stop=(c == 1))
                ins.then_inc(xz_acc, 1)
            for c in range(2):
                ins = mm(bank[1][0:SS, :], winz[:, c, :], xT[:, c, :], start=(c == 0), stop=(c == 1))
            ins.then_inc(xz_acc, 1)
            keep_warm(bank[3], WARM[3])
            pe.wait_ge(xc_ready, 1)
            mm(bank[4][:], cst[0:S, C_SEL:C_SEL + P], xc[0:S, 0, :], start=True, stop=True).then_inc(st_acc, 1)
            for k in range(KI):
                pe.wait_ge(xc_ready, k + 1)
                ins = mm(bank[2][:], wst[:, k, 0:2 * SS], xc[:, k, :], start=(k == 0), stop=(k == KI - 1))
            ins.then_inc(st_acc, 1)
            for k in range(KI):
                ins = mm(bank[3][0:SS, :], wst[:, k, 2 * SS:3 * SS], xc[:, k, :], start=(k == 0), stop=(k == KI - 1))
            ins.then_inc(st_acc, 1)
            keep_warm(bank[0], WARM[4])
            pe.wait_ge(g_ready, 1)
            for t in range(NT):
                mm(bank[(5 + t) % 8][:, 0:D], cz[:, t * P:(t + 1) * P], wout[:], start=True, stop=True).then_inc(ssm_acc, 1)

            keep_warm(bank[3], WARM[5])
            transpose_halves((bank[1], bank[2]), xh, ln_T, normalised(1))
            keep_warm(bank[3], WARM[6])
            pe.wait_ge(in_attn, 48)
            pe.wait_ge(xT_act, 2)
            pe.wait_ge(xT_dve, 2)
            for kind in range(2):
                for c in range(2):
                    at = kind * D + c * HALF
                    for k in range(2):
                        ins = mm(bank[3 + 2 * kind + c][0:HALF, :], qkvw[:, k, at:at + HALF], xT[:, k, :],
                                 start=(k == 0), stop=(k == 1))
                    ins.then_inc(qk_acc, 1)
            for t in range(NT):
                for k in range(2):
                    ins = mm(bank[(7, 0)[t // 2]][:, (t % 2) * D:(t % 2 + 1) * D], xT[:, k, t * P:(t + 1) * P],
                             qkvw[:, k, 2 * D:3 * D], start=(k == 0), stop=(k == 1))
                ins.then_inc(v_acc, 1)
            pe.wait_ge(cstb_ready, 1)
            for c in range(2):
                mm(bank[1 + c][0:HALF, :], cstb[0:HALF, C_ID:C_ID + HALF],
                   cstb[0:HALF, C_CM:C_CM + T].unsqueeze(1).to_broadcast([HALF, B, T]), start=True, stop=False,
                   skip_group_check=True)
                pe.wait_ge((qx_act, qx_dve)[c], 2)
                pe.wait_ge(kT_ready, c + 1)
                for b in range(B):
                    for i in range(PAIRS):
                        r = slice(i * PAIR, (i + 1) * PAIR)
                        ins = mm(bank[1 + c][r, b * T:(b + 1) * T], qx[r, c, b, :, :].rearrange("p h q -> p (h q)"),
                                 kT[r, c, b * T:(b + 1) * T], start=False, stop=(b == B - 1), skip_group_check=True,
                                 tile_position=(i * PAIR, i * PAIR))
                ins.then_inc(s_acc, 1)
            for c in range(2):
                pe.wait_ge(prob_ready, c + 1)
                for t in range(NT):
                    ins = nc.tensor.transpose(bank[3 + t][:, c * HALF:(c + 1) * HALF], prob[:, c, t * P:(t + 1) * P],
                                              ident[0:HALF, 0:HALF])
                    if c == 1:
                        ins.then_inc(p_T, 1)
            pe.wait_ge(ones_ready, 1)
            pe.wait_ge(v_ready, NT)
            for t in range(NT):
                pe.wait_ge(px_ready, t + 1)
                for hd in range(HEADS):
                    for i in range(P // PAIR):
                        r = slice(i * PAIR, (i + 1) * PAIR)
                        ins = mm(bank[(7 + t) % 8][r, hd * (DH + 1):(hd + 1) * (DH + 1)],
                                 px[r, t, hd, :, :].rearrange("p b q -> p (b q)"), v[r, t, hd, :], start=True, stop=True,
                                 tile_position=(i * PAIR, i * PAIR))
                ins.then_inc(o_acc, 1)
            transpose_halves((bank[3], bank[4]), o, o_T, lambda t: pe.wait_ge(o_ready, t + 1))
            pe.wait_ge(oT_act, 1)
            pe.wait_ge(oT_dve, 1)
            for t in range(NT):
                for k in range(2):
                    ins = mm(bank[(5 + t) % 8][:, 0:D], oT[:, k, t * P:(t + 1) * P], projw[:, k, :],
                             start=(k == 0), stop=(k == 1))
                ins.then_inc(x1_acc, 1)

            keep_warm(bank[3], WARM[7])
            transpose_halves((bank[1], bank[2]), xh, ln_T, normalised(2))
            pe.wait_ge(xT_act, 3)
            pe.wait_ge(xT_dve, 3)
            for t in range(NT):
                for k in range(2):
                    for j in range(QUAD):
                        at = t * P + j * REST
                        ins = mm(bank[3][j * REST:(j + 1) * REST, t * E:(t + 1) * E], xT[:, k, at:at + REST],
                                 gatew[:, k, :], start=(k == 0), stop=(k == 1), tile_position=(0, j * REST))
            ins.then_inc(lg_acc, 1)
            keep_warm(bank[4], WARM[8])
            pe.wait_ge(hotb_ready, 1)
            flat = hotb[:, :, :].rearrange("p j e -> p (j e)")
            mm(bank[4][:, 0:J * E], cstb[:, C_TRI:C_TRI + P], flat, start=True, stop=False, skip_group_check=True)
            for j in range(J - 1):
                ins = mm(bank[4][:, (j + 1) * E:J * E], cstb[:, C_ONE:C_ONE + P],
                         hotb[:, j:j + 1, :].to_broadcast([P, J - 1 - j, E]), start=False, stop=(j == J - 2),
                         skip_group_check=True)
            ins.then_inc(pos_acc, 1)

            def dispatch(e):
                to = bank[5 + e % 2]
                if e == 0:
                    pe.wait_ge(part_act, 2)
                    pe.wait_ge(part_pool, 2)
                if e >= 2:
                    pe.wait_ge(xbT_ready, 2 * (e - 1))
                    pe.wait_ge(put_sum, 2 * (e - 1))
                pe.wait_ge(oh_ready, NT * (e + 1))
                for c in range(2):
                    for part in range(PARTS):
                        for t in range(NT):
                            ins = mm(to[0:HALF, c * CAP:(c + 1) * CAP], parts[:, part, t, c * HALF:(c + 1) * HALF],
                                     oh[:, e % 2, t, :], start=(part == 0 and t == 0),
                                     stop=(part == PARTS - 1 and t == NT - 1))
                j = e % QUAD
                at = 2 * CAP
                for t in range(NT):
                    mm(to[:, at:at + 3], oh[:, e % 2, t, 0:P], token[:, t, e, :], start=(t == 0), stop=(t == NT - 1))
                for t in range(NT):
                    ins = mm(to[j * REST:(j + 1) * REST, at + 4:at + 7], oh[:, e % 2, t, P:CAP], token[:, t, e, :],
                             start=(t == 0), stop=(t == NT - 1), tile_position=(0, j * REST))
                ins.then_inc(xb_acc, 1)

            def hidden(e):
                pe.wait_ge(xbT_ready, 2 * (e + 1))
                pe.wait_ge(in_fc[e], 16)
                if e >= 2:
                    pe.wait_ge(hid_ready, KF * (e - 1))
                for f in range(KF):
                    to = bank[2 * (e % 2) + f // (KF // 2)][:, f % (KF // 2) * CAP:(f % (KF // 2) + 1) * CAP]
                    for c in range(2):
                        ins = mm(to, fcw[:, e, c, f * P:(f + 1) * P], xbT[:, e % 2, c, :], start=(c == 0), stop=(c == 1))
                    if f % (KF // 2) == KF // 2 - 1:
                        ins.then_inc(fc_acc, 1)

            def project(n):
                first_e, last_e = OUTPUTS[n]
                to = bank[(4, 7)[n % 2]]
                for e in range(first_e, last_e + 1):
                    pe.wait_ge(in_pj[e], 16)
                pe.wait_ge(hid_ready, KF * (last_e + 1))
                if n >= 2:
                    pe.wait_ge(y_ready, n - 1)
                for f in range(KF):
                    if first_e == last_e:
                        ins = mm(to[:, 0:D], hid[:, first_e % HB, f, 0:P], pjw[:, first_e, f, :],
                                 start=(f == 0), stop=(f == KF - 1))
                    else:
                        for j in range(QUAD):
                            e = first_e + j
                            ins = mm(to[j * REST:(j + 1) * REST, 0:D], hid[:, e % HB, f, P:CAP], pjw[:, e, f, :],
                                     start=(f == 0), stop=(f == KF - 1), tile_position=(0, j * REST))
                ins.then_inc(pj_acc, 1)

            pe.wait_ge(token_ready, 1)
            dispatch(0)
            for e in range(E):
                if e + 1 < E:
                    dispatch(e + 1)
                hidden(e)
                for n, (_, last_e) in enumerate(OUTPUTS):
                    if last_e == e - 1:
                        project(n)
            for n, (_, last_e) in enumerate(OUTPUTS):
                if last_e == E - 1:
                    project(n)

        @block.vector
        def _(dve):
            V = nc.vector
            steps, sums = [0], [0]

            def step(ins):
                steps[0] += 1
                ins.then_inc(dve_step, 1)
                dve.wait_ge(dve_step, steps[0])

            norms = [0]

            def layer_norm(src, to, both=False, added=None):
                for t in range(NT):
                    if added:
                        added(t)
                    ins = V.bn_stats(st[:, t, :], src[:, t, :])
                step(ins)
                for t in range(NT):
                    ins = V.bn_aggr(mv[:, t, :], st[:, t, :])
                step(ins)
                if both:
                    V.tensor_scalar(ve[:, 0:NT], mv[:, :, 1], 1.0 + EPS, EPS * EPS, ALU.mult, ALU.add)
                    V.tensor_scalar(ve[:, NT:2 * NT], mv[:, :, 1], EPS, None, ALU.add).then_inc(var_ready, 1)
                else:
                    V.tensor_scalar(ve[:, 0:NT], mv[:, :, 1], EPS, None, ALU.add).then_inc(var_ready, 1)
                norms[0] += 1
                dve.wait_ge(rstd_ready, norms[0])
                for t in range(NT - 1):
                    V.tensor_scalar(to[:, t, :], src[:, t, :], mv[:, t, 0:1], rstd[:, t:t + 1],
                                    ALU.subtract, ALU.mult).then_inc(ln_ready, 1)

            dve.wait_ge(in_rows, 16)
            def add_b(t):
                dve.wait_ge(tok_acc, t + 1)
                V.tensor_tensor(h[:, t, :], bank[t][:, 0:D], row[:, 0, :], ALU.add).then_inc(h_ready, 1)
                dve.wait_ge(h_ready, t + 1)

            layer_norm(h, xh, added=add_b)
            dve.wait_ge(in_small, 48)
            dve.wait_ge(in_cst, 16)
            V.tensor_scalar(ndtb[:], spt[0:SS, SP_DT:SP_DT + 1], -1.0, None, ALU.mult).then_inc(small_ready, 1)
            cw = ppt[:, PP_CW:PP_CW + KI * TAPS].rearrange("p (m s) -> p m s", m=KI)[:, :, TAPS - 1]
            V.tensor_tensor(bcw[:], ppt[:, PP_BIN:PP_BIN + KI], cw, ALU.mult).then_inc(bcw_ready, 1)
            dve.wait_ge(ln_T, 2)
            V.tensor_copy(xT[:, 1, :], bank[5][0:HALF, :]).then_inc(xT_dve, 1)
            V.tensor_scalar(qbm[:], hmask, qpt[:, QP_QB:QP_QB + 1], None, ALU.mult).then_inc(small_ready, 1)

            for m in range(KI):
                dve.wait_ge(conv_in, 2 * (m + 1))
                tap = PP_CW + m * TAPS
                xv = conv[:, 0, m, :].rearrange("p (b t) -> p b t", b=B)
                sv = conv[:, 1, m, :].rearrange("p (b t) -> p b t", b=B)
                for s in range(1, TAPS):
                    ins = V.scalar_tensor_tensor(sv[:, :, s:T], xv[:, :, 0:T - s], ppt[:, tap + TAPS - 1 - s:tap + TAPS - s],
                                                 sv[:, :, s:T], ALU.mult, ALU.add)
                    if s < TAPS - 1:
                        step(ins)
                ins.then_inc(conv_out, 1)
            dve.wait_ge(xrep_ready, 1)
            dve.wait_ge(st_acc, 2)
            V.scalar_tensor_tensor(bx[:], bank[2][SS:2 * SS, :], spt[SS:2 * SS, SP_DT:SP_DT + 1], xrep[SS:2 * SS, :],
                                   ALU.add, ALU.mult)
            dve.wait_ge(decay_ready, 1)
            step(V.memset(decay[:].rearrange("p (b t) -> p b t", b=B)[:, :, 0:1], 0.0))
            step(V.tensor_tensor_scan(hs, decay[:], bx[:], 0.0, ALU.mult, ALU.add))
            dve.wait_ge(st_acc, 3)
            dve.wait_ge(sz_ready, 1)
            step(V.scalar_tensor_tensor(cz[:], bank[3][0:SS, :], spt[0:SS, SP_C:SP_C + 1], sz[:], ALU.add, ALU.mult))
            V.tensor_tensor(cz[:], hs, cz[:], ALU.mult).then_inc(g_ready, 1)
            dve.wait_ge(hb_ready, 1)
            def add_ssm(t):
                dve.wait_ge(ssm_acc, t + 1)
                V.tensor_tensor(h2[:, t, :], bank[(5 + t) % 8][:, 0:D], h[:, t, :], ALU.add).then_inc(h2_ready, 1)
                dve.wait_ge(h2_ready, t + 1)

            layer_norm(h2, xh, both=True, added=add_ssm)

            dve.wait_ge(ln_T, 4)
            V.tensor_scalar(xT[:, 1, :], bank[2][0:HALF, :], qpt[:, QP_L1W + 1:QP_L1W + 2], qpt[:, QP_L1B + 1:QP_L1B + 2],
                            ALU.mult, ALU.add).then_inc(xT_dve, 1)
            dve.wait_ge(qk_acc, 2)
            for a in range(2):
                V.tensor_scalar(qx[:, 1, :, a, :], bank[4][0:HALF, :].rearrange("p (b q) -> p b q", b=B),
                                qpt[:, QP_QB + 1:QP_QB + 2], hmask[:, a:a + 1], ALU.add, ALU.mult).then_inc(qx_dve, 1)
            for t in range(NT):
                dve.wait_ge(v_acc, 2 * (t // 2) + 2)
                V.tensor_tensor(v[:, t, :, 0:DH], bank[(7, 0)[t // 2]][:, (t % 2) * D:(t % 2 + 1) * D].rearrange(
                    "p (h d) -> p h d", h=HEADS), row[:, 2, :].rearrange("p (h d) -> p h d", h=HEADS),
                    ALU.add).then_inc(v_ready, 1)
            for c in range(2):
                dve.wait_ge(s_acc, c + 1)
                scores = bank[1 + c][0:HALF, :].rearrange("p (b k) -> p b k", b=B)
                step(V.tensor_reduce(nmax[:, c, :], scores, AX_X, ALU.max))
                V.tensor_tensor(prob[:, c, :].rearrange("p (b k) -> p b k", b=B), scores,
                                nmax[:, c, :].unsqueeze(2).to_broadcast([HALF, B, T]), ALU.subtract).then_inc(shifted, 1)
            for t in range(NT):
                dve.wait_ge(p_T, t + 1)
                V.tensor_tensor(px[:, t, :, :, :],
                                bank[3 + t][:, 0:D].rearrange("p (h q) -> p h q", h=HEADS).unsqueeze(2).to_broadcast(
                                    [P, HEADS, 2, T]),
                                bmask.unsqueeze(1).unsqueeze(3).to_broadcast([P, HEADS, 2, T]),
                                ALU.mult).then_inc(px_ready, 1)
            for t in range(NT):
                dve.wait_ge(o_acc, t + 1)
                ot = bank[(7 + t) % 8][:, 0:HEADS * (DH + 1)].rearrange("p (h d) -> p h d", h=HEADS)
                step(V.reciprocal(den[:, t, :], ot[:, :, DH]))
                V.tensor_tensor(o[:, t, :].rearrange("p (h d) -> p h d", h=HEADS), ot[:, :, 0:DH],
                                den[:, t, :].unsqueeze(2).to_broadcast([P, HEADS, DH]), ALU.mult).then_inc(o_ready, 1)
            dve.wait_ge(o_T, 2)
            V.tensor_copy(oT[:, 1, :], bank[4][0:HALF, :]).then_inc(oT_dve, 1)
            dve.wait_ge(xpb_ready, 1)

            def add_attention(t):
                dve.wait_ge(x1_acc, t + 1)
                V.tensor_tensor(x1[:, t, :], bank[(5 + t) % 8][:, 0:D], xp[:, t, :], ALU.add).then_inc(x1_ready, 1)
                dve.wait_ge(x1_ready, t + 1)

            layer_norm(x1, xh, added=add_attention)

            dve.wait_ge(ln_T, 6)
            V.tensor_scalar(xT[:, 1, :], bank[2][0:HALF, :], qpt[:, QP_L2W + 1:QP_L2W + 2], qpt[:, QP_L2B + 1:QP_L2B + 2],
                            ALU.mult, ALU.add).then_inc(xT_dve, 1)
            dve.wait_ge(lg_acc, 1)
            for t in range(NT):
                ins = V.max(top[:, t, :], bank[3][:, t * E:(t + 1) * E])
            step(ins)
            for t in range(NT):
                ins = V.max_index(chosen[:, t, :], top[:, t, :], bank[3][:, t * E:(t + 1) * E])
            step(ins)
            for k in range(TOPK):
                ins = V.tensor_tensor(hotb[:, k * NT:(k + 1) * NT, :],
                                      cst[:, C_CHOICE:C_CHOICE + NT * E].rearrange("p (t e) -> p t e", t=NT),
                                      chosen[:, :, k:k + 1].to_broadcast([P, NT, E]), ALU.is_equal)
            ins.then_inc(hotb_ready, 1)
            V.tensor_tensor(gap[:], top[:, :, 0], top[:, :, 1], ALU.subtract).then_inc(gap_ready, 1)
            dve.wait_ge(hotb_ready, 1)
            V.scalar_tensor_tensor(token[:, :, :, 2], hotb[:, NT:J, :], float(N), token[:, :, :, 2],
                                   ALU.mult, ALU.add).then_inc(token_ready, 1)
            step(V.tensor_tensor(miss[:], hotb[:, 0:NT, :], hotb[:, NT:J, :], ALU.add))
            step(V.tensor_scalar(miss[:], miss[:], -NOWHERE, NOWHERE, ALU.mult, ALU.add))
            dve.wait_ge(pos_acc, 1)
            step(V.tensor_tensor(pos[:], bank[4][:, 0:J * E].rearrange("p (j e) -> p j e", j=J), hotb[:], ALU.mult))
            step(V.tensor_tensor(place[:], pos[:, 0:NT, :], pos[:, NT:J, :], ALU.add))
            step(V.tensor_tensor(place[:], place[:], miss[:], ALU.add))

            def one_hot(e):
                if e >= 2:
                    dve.wait_ge(xb_acc, e - 1)
                for t in range(NT):
                    V.tensor_scalar(oh[:, e % 2, t, :], cstb[:, C_SLOT:C_SLOT + CAP], place[:, t, e:e + 1], None,
                                    ALU.is_equal).then_inc(oh_ready, 1)

            def affine(e):
                dve.wait_ge(xb_acc, e + 1)
                if e >= 2:
                    dve.wait_ge(fc_acc, 2 * (e - 1))
                for c in range(2):
                    V.tensor_scalar(xbT[:, e % 2, c, :], bank[5 + e % 2][0:HALF, c * CAP:(c + 1) * CAP],
                                    qpt[:, QP_L2W + c:QP_L2W + c + 1], qpt[:, QP_L2B + c:QP_L2B + c + 1],
                                    ALU.mult, ALU.add).then_inc(xbT_ready, 1)

            def rows_of_slots(e):
                j = e % QUAD
                for n, r, at in ((OUTPUTS.index((e, e)), slice(0, P), 2 * CAP),
                                 (OUTPUTS.index((e - j, e - j + QUAD - 1)), slice(j * REST, (j + 1) * REST), 2 * CAP + 4)):
                    to = bank[5 + e % 2]
                    V.tensor_copy(row_of[r, n, 0:3], to[r, at:at + 3]).then_inc(put_sum, 1)
                    sums[0] += 1
                    dve.wait_ge(put_sum, sums[0])
                    step(V.scalar_tensor_tensor(row_of[r, n, 3:4], row_of[r, n, 1:2], cst[r, C_NHOLE + n:C_NHOLE + n + 1],
                                                row_of[r, n, 0:1], ALU.mult, ALU.add))
                    ins = V.scalar_tensor_tensor(put[r, n:n + 1], row_of[r, n, 2:3], cst[r, C_HOLE + n:C_HOLE + n + 1],
                                                 row_of[r, n, 3:4], ALU.add, ALU.add)
                    if r.stop - r.start == P or j == QUAD - 1:
                        ins.then_inc(put_ready, 1)

            def outputs(n):
                dve.wait_ge(pj_acc, n + 1)
                first_e, last_e = OUTPUTS[n]
                own = first_e if first_e == last_e else E + first_e // QUAD
                V.tensor_tensor(y_rows[:, n, :], bank[(4, 7)[n % 2]][:, 0:D], pjb[:, own, :], ALU.add).then_inc(y_ready, 1)

            one_hot(0)
            one_hot(1)
            affine(0)
            rows_of_slots(0)
            dve.wait_ge(in_pjb, 16 * (E + 1))
            for e in range(E):
                if e + 2 < E:
                    one_hot(e + 2)
                if e + 1 < E:
                    affine(e + 1)
                    rows_of_slots(e + 1)
                for n, (_, last_e) in enumerate(OUTPUTS):
                    if last_e == e - 1:
                        outputs(n)
            for n, (_, last_e) in enumerate(OUTPUTS):
                if last_e == E - 1:
                    outputs(n)
            dve.wait_ge(wgt_ready, 2)
            dve.wait_ge(base_ready, 1)
            for t in range(NT):
                dve.wait_ge(gathered[t], 16)
                step(V.scalar_tensor_tensor(h2[:, t, :], got[:, t, :], wgt[:, t:t + 1], h2[:, t, :], ALU.mult, ALU.add))
                V.scalar_tensor_tensor(h2[:, t, :], got[:, NT + t, :], wgt[:, NT + t:NT + t + 1], h2[:, t, :],
                                       ALU.mult, ALU.add).then_inc(res_ready, 1)


def kernel(x, L0_tok_W, L0_tok_b, L0_attn_W_in, L0_attn_b_in, L0_attn_conv_w, L0_attn_conv_b, L0_attn_W_x,
           L0_attn_b_x, L0_attn_W_dt, L0_attn_b_dt, L0_attn_W_out, L0_attn_b_out, L0_ffn_ln1_w, L0_ffn_ln1_b,
           L0_ffn_ln2_w, L0_ffn_ln2_b, L0_ffn_attn_qkv_w, L0_ffn_attn_qkv_b, L0_ffn_attn_proj_w,
           L0_ffn_attn_proj_b, L0_ffn_w_g, L0_ffn_exp_fc_w, L0_ffn_exp_fc_b, L0_ffn_exp_proj_w,
           L0_ffn_exp_proj_b):
    import concourse.bacc as bacc
    from concourse.bass_utils import run_bass_kernel_spmd

    def a(v):
        return np.asarray(v)

    def halves(w):
        return a(w).reshape(2, HALF, -1).transpose(1, 0, 2)

    def chunks(w):
        w = a(w)
        return w.reshape(w.shape[0] // P, P, -1).transpose(1, 0, 2)

    def by_j(w):
        return np.tile(w, S)

    def by_i(w):
        return np.repeat(w, S, axis=-1)

    side = x.shape[-1] // 4
    patches = a(x).reshape(B, 3, 4, side, 4, side).transpose(3, 5, 1, 0, 2, 4).reshape(PIX, N)
    b_dt, b_x, b_in = a(L0_attn_b_dt), a(L0_attn_b_x), a(L0_attn_b_in)
    w_x, qkv_b = a(L0_attn_W_x), a(L0_ffn_attn_qkv_b)
    pp = np.concatenate([
        b_in[:INNER].reshape(KI, P).T,
        a(L0_attn_conv_w).reshape(KI, P, TAPS).transpose(1, 0, 2).reshape(P, KI * TAPS),
        a(L0_attn_conv_b).reshape(KI, P).T,
        a(L0_ffn_exp_fc_b).reshape(E, KF, P).transpose(2, 0, 1).reshape(P, E * KF)], axis=1)
    qp = np.concatenate([a(v).reshape(2, HALF).T for v in (
        L0_ffn_ln1_w, L0_ffn_ln1_b, L0_ffn_ln2_w, L0_ffn_ln2_b, qkv_b[:D], qkv_b[D:2 * D])], axis=1)
    state_b = np.stack([
        np.concatenate([by_j(b_dt[:S]), by_j(b_x[2 * S:3 * S])]),
        np.concatenate([by_j(b_x[3 * S:4 * S])] * 2),
        np.concatenate([by_i(b_in[INNER:WIN])] * 2)], axis=1)
    data = {
        "patches": patches.reshape(KP, P, N).transpose(1, 0, 2),
        "tok_w": chunks(a(L0_tok_W).T),
        "w_in": halves(a(L0_attn_W_in)[:, :INNER]),
        "w_z": halves(by_i(a(L0_attn_W_in)[:, INNER:WIN])),
        "w_state": chunks(np.concatenate([by_j(a(L0_attn_W_dt)[:, :S]), by_j(w_x[:, 2 * S:3 * S]),
                                          by_j(w_x[:, 3 * S:4 * S])], axis=1)),
        "w_out": np.repeat(a(L0_attn_W_out)[:S], S, axis=0),
        "qkv_w": halves(L0_ffn_attn_qkv_w),
        "proj_w": halves(L0_ffn_attn_proj_w),
        "gate_w": halves(L0_ffn_w_g),
        "fc_w": a(L0_ffn_exp_fc_w).reshape(E, 2, HALF, F).transpose(2, 0, 1, 3),
        "pj_w": a(L0_ffn_exp_proj_w).reshape(E, KF, P, D).transpose(2, 0, 1, 3),
        "pp": pp,
        "qp": qp,
        "sp_par": state_b,
        "rows": np.stack([a(L0_tok_b), a(L0_attn_b_out), qkv_b[2 * D:], a(L0_ffn_attn_proj_b)]),
        "pj_b": a(L0_ffn_exp_proj_b).reshape(E, D),
        "consts": constants(),
    }
    nc = bacc.Bacc("TRN2", target_bir_lowering=False, num_devices=1)
    arrays, args = {}, []
    for name, v in data.items():
        v = np.ascontiguousarray(v)
        arrays[f"in_{name}"] = v
        args.append(nc.dram_tensor(f"in_{name}", v.shape, mybir.dt.from_np(v.dtype), kind="ExternalInput").ap())
    args.append(nc.dram_tensor("out_0_dram", (N, D), F32, kind="ExternalOutput").ap())
    vit_block(nc, *args)
    r = run_bass_kernel_spmd(nc, [arrays], core_ids=[0])
    return r.results[0]["out_0_dram"].reshape(B, T, D)
```

```python
from contextlib import ExitStack

import numpy as np

import concourse.bass as bass
from concourse import mybir
from concourse.alu_op_type import AluOpType as ALU

F32 = mybir.dt.float32
BF16 = mybir.dt.bfloat16
I32 = mybir.dt.int32
ACT = mybir.ActivationFunctionType
AX_X = mybir.AxisListType.X

P = 128
B, T = 32, 16
N = B * T
NT = N // P
BT = P // T
D = 192
HALF = D // 2
PIX = 768
KP = PIX // P
PIECES = 6
INNER = 384
KI = INNER // P
S = 8
SS = S * S
TAPS = 4
HEADS, DH = 12, 16
HH = HEADS // 2
PAIR = 2 * DH
PAIRS = HALF // PAIR
U = 2
UB, UN = B // U, N // U
UT = NT // U
IP = P // PAIR
E, TOPK = 8, 2
CAP = 160
CAP += CAP % 2
assert CAP == int(TOPK * 1.25 * N / E)
M2 = CAP // 2
QUAD = 4
REST = CAP - P
assert REST * QUAD == P
HB = 5
F = 768
KF = F // P
J = TOPK * NT
EPS = 1e-5
NEG = -1.0e30
ZERO = 256
WIN = INNER + S

PP_BIN, PP_CW, PP_CB, PP_FCB = 0, KI, KI + KI * TAPS, 2 * KI + KI * TAPS
PP_W = PP_FCB + E * KF
QP_L1W, QP_L1B, QP_L2W, QP_L2B, QP_QB, QP_KB, QP_W = 0, 2, 4, 6, 8, 10, 12
SP_DT, SP_C, SP_Z, SP_W = 0, 1, 2, 3
C_ID, C_TRI, C_ONE = 0, P, 2 * P
C_CM = 3 * P
C_TOKEN = C_CM + T
C_SLOT = C_TOKEN + NT * E * 3
C_BF = C_SLOT + CAP
C_HM = C_BF
C_BM = C_HM + 2
C_CHOICE = C_BM + 2
C_HALF = C_CHOICE + J * E
C_HOLE = C_HALF + NT
C_NHOLE = C_HOLE + E + E // QUAD
C_W = C_NHOLE + E + E // QUAD
PARTS = 3
NOWHERE = 1000.0

OUTPUTS = []
for e in range(E):
    OUTPUTS.append((e, e))
    if e % QUAD == QUAD - 1:
        OUTPUTS.append((e - QUAD + 1, e))
SENT = len(OUTPUTS) - 2


WARM = (19, 10, 0, 2, 3, 12, 1, 0, 5, 1, 0, 11, 3, 0, 0, 2, 0, 7, 9, 4)
IDLE0, IDLE1 = (), (0, 22, 25, 27)
O_BANK = ((7, 0, 3, 4), (1, 2, 5, 6))
T_BANK = (((4, 5), (2, 3)), ((1, 2), (7, 0)), ((1, 2), (5, 6)))
H2_BANK = (5, 6, 7, 0)
PT_BANK = (5, 6, 6, 5)
X1_BANK = (7, 0, 3, 4)


def constants():
    c = np.zeros((P, C_W), np.float32)
    p = np.arange(P)
    c[:, C_ID:C_ID + P] = np.eye(P)
    c[:, C_TRI:C_TRI + P] = p[:, None] < p[None, :]
    c[:, C_ONE:C_ONE + P] = 1.0
    c[:HALF, C_CM:C_CM + T] = np.where(np.arange(T)[None, :] <= (p[:HALF] % T)[:, None], 0.0, NEG)
    c[:, C_BM:C_BM + 2] = p[:, None] // T % 2 == np.arange(2)[None, :]
    c[:, C_HM:C_HM + 2] = c[:, C_BM:C_BM + 2] * DH ** -0.5
    token = c[:, C_TOKEN:C_TOKEN + NT * E * 3].reshape(P, NT, E, 3)
    token[..., 0] = p[:, None, None]
    token[..., 1] = 1.0
    token[..., 2] = np.arange(NT)[None, :, None] * P
    c[:, C_TOKEN:C_TOKEN + NT * E * 3] = token.reshape(P, -1)
    c[:, C_SLOT:C_SLOT + CAP] = np.arange(CAP)
    c[:, C_CHOICE:C_CHOICE + J * E] = np.tile(np.arange(E), J)
    hole = J * P + np.arange(len(OUTPUTS))[None, :] * P + p[:, None]
    c[:, C_HOLE:C_HOLE + len(OUTPUTS)] = hole
    c[:, C_NHOLE:C_NHOLE + len(OUTPUTS)] = -hole
    c[:, C_HALF:C_HALF + NT] = -0.5
    return c


def vit_block(nc, patches, tok_w, w_in, w_z, w_state, w_out, qkv_w, proj_w, gate_w, fc_w, pj_w,
              pp, qp, sp_par, rows, pj_b, consts, out):
    ctx = ExitStack()
    with ctx:
        def sb(name, shape, dt=F32):
            return ctx.enter_context(nc.sbuf_tensor(name, shape, dt))

        def sem(name):
            return ctx.enter_context(nc.semaphore(name))

        choice_out = nc.dram_tensor("choice_out", (J * P + SENT * P, D), F32).ap()

        bank = [ctx.enter_context(nc.psum_tensor(f"bank{i}", [P, 512], F32)) for i in range(8)]

        cst = sb("cst", [P, C_W])
        cstb = sb("cstb", [P, C_BF], BF16)
        ppt = sb("ppt", [P, PP_W])
        qpt = sb("qpt", [HALF, QP_W])
        spt = sb("spt", [P, SP_W])
        row = sb("row", [P, 4, D])
        pjb = sb("pjb", [P, E + E // QUAD, D])
        pat = sb("pat", [P, KP, N])
        tokw = sb("tokw", [P, KP, D])
        win = sb("win", [HALF, 2, INNER])
        winz = sb("winz", [HALF, 2, SS])
        wst = sb("wst", [P, KI, 4 * SS])
        wout = sb("wout", [SS, D])
        qkvw = sb("qkvw", [HALF, 2, 3 * D])
        projw = sb("projw", [HALF, 2, D])
        gatew = sb("gatew", [HALF, 2, E])
        fcw = sb("fcw", [HALF, E, 2, F])
        pjw = sb("pjw", [P, E, KF, D])
        zeros = sb("zeros", [P, ZERO])

        h = sb("h", [P, NT, D])
        h2 = sb("h2", [P, NT, D])
        xh = sb("xh", [P, NT, D])
        xp = sb("xp", [P, NT, D])
        x1 = sb("x1", [P, NT, D])
        st = sb("st", [P, NT, 6])
        mv = sb("mv", [P, NT, 2])
        ve = sb("ve", [P, 2 * NT])
        rstd = sb("rstd", [P, 2 * NT])
        xT = sb("xT", [HALF, 2, N])
        conv = sb("conv", [P, 2, KI, N])
        xc = sb("xc", [P, KI, N])
        ndtb = sb("ndtb", [SS, 1])
        sz = sb("sz", [SS, N])
        xrep = sb("xrep", [P, N])
        decay = sb("decay", [SS, N])
        bx = sb("bx", [SS, N])
        cz = sb("cz", [SS, N])
        hs = conv[0:SS, 0, 0, :]
        qbm = sb("qbm", [HALF, 2])
        kT = sb("kT", [HALF, 2, N])
        hid = sb("hid", [P, HB, KF, CAP])
        flat_hid = hid[:, :, :, :].rearrange("p b f s -> p (b f s)")
        qx = flat_hid[0:HALF, 0:4 * N].rearrange("p (c b a q) -> p c b a q", c=2, b=B, a=2)
        px = flat_hid[:, 4 * N:4 * N + NT * HEADS * 2 * T].rearrange("p (t h a q) -> p t h a q", t=NT, h=HEADS, a=2)
        v = sb("v", [P, NT, D])
        top_score = sb("top_score", [HALF, 2 * UB])
        total = sb("total", [HALF, U, 2 * UB])
        prob = xc[0:HALF, 0:U, :]
        o_half = tokw[0:HALF, :, :].rearrange("p k d -> p (k d)")[:, 0:2 * N].rearrange(
            "p (u i n) -> p u i n", u=U, i=IP)
        oT = xT[:, :, :].rearrange("p c n -> p (c n)").rearrange("p (k i n) -> p k i n", k=2 * NT, i=IP)
        top = sb("top", [P, NT, 8])
        chosen = sb("chosen", [P, NT, 8], mybir.dt.uint32)
        hotb = sb("hotb", [P, J, E], BF16)
        gap = sb("gap", [P, NT])
        wgt = sb("wgt", [P, J])
        pos = sb("pos", [P, J, E])
        miss = sb("miss", [P, NT, E])
        place = sb("place", [P, NT, E])
        oh = sb("oh", [P, 2, NT, CAP], BF16)
        row_of = sb("row_of", [P, len(OUTPUTS), 4])
        put = sb("put", [P, SENT], I32)
        slot_token = sb("slot_token", [P, 2])
        in_tile = sb("in_tile", [P, 2, NT])
        slot_share = sb("slot_share", [P, 2])
        share = sb("share", [P, NT, QUAD])
        share2 = sb("share2", [P, NT, QUAD])
        share_part = sb("share_part", [P, PARTS, NT, QUAD], BF16)
        comb = xc[:, 0:2, :]
        bcw = sb("bcw", [P, KI])
        got = pat[:, 0:3, :].rearrange("p a b -> p (a b)").rearrange("p (j d) -> p j d", j=J)
        left = tokw[:, 0:NT, :]
        parts = pat[:, 3:KP, :].rearrange("p a b -> p (a b)").bitcast(BF16)[:, 0:PARTS * NT * D].rearrange(
            "p (n t d) -> p n t d", n=PARTS, t=NT)

        flat_conv = conv[:, :, :, :].rearrange("p x a b -> p (x a b)")
        xbT = flat_conv[0:HALF, len(OUTPUTS) * D:len(OUTPUTS) * D + 4 * CAP].rearrange("p (b c s) -> p b c s", b=2, c=2)
        y_rows = conv[:, :, :, :].rearrange("p x a b -> p (x a b)")[:, 0:len(OUTPUTS) * D].rearrange(
            "p (n d) -> p n d", d=D)
        token = cstb[:, C_TOKEN:C_TOKEN + NT * E * 3].rearrange("p (t e n) -> p t e n", t=NT, e=E)
        zeros_b = zeros[:].bitcast(BF16)
        ident = cst[:, C_ID:C_ID + P]
        hmask = cst[0:HALF, C_HM:C_HM + 2]
        bmask = cst[:, C_BM:C_BM + 2]

        in_tok = [sem(f"in_tok{i}") for i in range(PIECES)]
        in_cst, in_small, in_ssm, in_rows, in_attn, in_zero = (sem(n) for n in (
            "in_cst", "in_small", "in_ssm", "in_rows", "in_attn", "in_zero"))
        in_fc = [sem(f"in_fc{e}") for e in range(E)]
        in_pj = [sem(f"in_pj{e}") for e in range(E)]
        in_pjb = sem("in_pjb")
        zeros_ready, zero_rows = sem("zeros_ready"), sem("zero_rows")
        cstb_ready = sem("cstb_ready")
        tok_acc, ln_T, xz_acc, st_acc, ssm_acc, qk_acc, v_acc, s_acc, p_T, o_acc, x1_acc = (sem(n) for n in (
            "tok_acc", "ln_T", "xz_acc", "st_acc", "ssm_acc", "qk_acc", "v_acc", "s_acc", "p_T", "o_acc", "x1_acc"))
        lg_acc, pos_acc, xb_acc, fc_acc, pj_acc = (sem(n) for n in ("lg_acc", "pos_acc", "xb_acc", "fc_acc", "pj_acc"))
        ln_ready, xT_act, xT_dve, conv_in, conv_out, xc_ready, small_ready = (sem(n) for n in (
            "ln_ready", "xT_act", "xT_dve", "conv_in", "conv_out", "xc_ready", "small_ready"))
        sz_ready, xrep_ready, decay_ready, g_ready, hb_ready, h_ready = (sem(n) for n in (
            "sz_ready", "xrep_ready", "decay_ready", "g_ready", "hb_ready", "h_ready"))
        qx_act, qx_dve, kT_act, kT_dve, v_ready, shifted, exp_ready, prob_ready, px_act, px_dve, o_ready, oT_ready = (
            sem(n) for n in ("qx_act", "qx_dve", "kT_act", "kT_dve", "v_ready", "shifted", "exp_ready", "prob_ready",
                             "px_act", "px_dve", "o_ready", "oT_ready"))
        xpb_ready, h2_ready, base_ready, gap_ready, wgt_ready, hotb_ready, put_ready, oh_ready = (sem(n) for n in (
            "xpb_ready", "h2_ready", "base_ready", "gap_ready", "wgt_ready", "hotb_ready", "put_ready",
            "oh_ready"))
        part_act, part_pool, bcw_ready, token_ready = (sem(n) for n in ("part_act", "part_pool", "bcw_ready", "token_ready"))
        scattered, xbT_ready, hid_ready, y_ready, res_ready, stored = (
            sem(n) for n in ("scattered", "xbT_ready", "hid_ready", "y_ready", "res_ready", "stored"))
        gathered = [sem(f"gathered{t}") for t in range(NT)]
        dve_step, pool_step = sem("dve_step"), sem("pool_step")
        choice_added, xrep_acc, c_acc = sem("choice_added"), sem("xrep_acc"), sem("c_acc")
        share_ready, comb_ready, comb_acc = sem("share_ready"), sem("comb_ready"), sem("comb_acc")
        x1_ready, put_sum, stats_ready = sem("x1_ready"), sem("put_sum"), sem("stats_ready")
        var_ready, rstd_ready = sem("var_ready"), sem("rstd_ready")

        def pT(t):
            return bank[PT_BANK[t]][:, 0:D].rearrange("p (h q) -> p h q", h=HEADS)

        block = ctx.enter_context(nc.Block())

        @block.sync
        def _(sync):
            for i in range(PIECES):
                k = slice(i * KP // PIECES, (i + 1) * KP // PIECES)
                sync.dma_start(pat[:, k, :], patches[:, k, :]).then_inc(in_tok[i], 16)
            sync.dma_start(win[:], w_in).then_inc(in_ssm, 16)
            sync.dma_start(winz[:], w_z).then_inc(in_ssm, 16)
            sync.dma_start(wst[:], w_state).then_inc(in_ssm, 16)
            sync.dma_start(wout[:], w_out).then_inc(in_ssm, 16)
            sync.dma_start(qkvw[:], qkv_w).then_inc(in_attn, 16)
            sync.dma_start(projw[:], proj_w).then_inc(in_attn, 16)
            sync.dma_start(gatew[:], gate_w).then_inc(in_attn, 16)
            sync.wait_ge(zeros_ready, 1)
            sync.dma_start(choice_out[0:J * P, :].rearrange("(p n) d -> p (n d)", p=P).rearrange(
                "p (r z) -> p r z", z=ZERO), zeros[:].unsqueeze(1).to_broadcast([P, J * D // ZERO, ZERO])).then_inc(
                    zero_rows, 16)
            for e in range(E):
                sync.dma_start(fcw[:, e, :, :], fc_w[:, e, :, :]).then_inc(in_fc[e], 16)
                sync.dma_start(pjw[:, e, :, :], pj_w[:, e, :, :]).then_inc(in_pj[e], 16)
            sync.dma_start(pjb[:, 0:E, :], pj_b.partition_broadcast(P)).then_inc(in_pjb, 16)
            for e in range(E):
                j = e % QUAD
                sync.dma_start(pjb[j * REST:(j + 1) * REST, E + e // QUAD, :],
                              pj_b[e, :].partition_broadcast(REST)).then_inc(in_pjb, 16)
            sync.wait_ge(scattered, 16 * SENT)
            for t in range(NT):
                sync.dma_start(got[:, t:J:NT, :], choice_out[0:J * P, :].rearrange("(j p) d -> p j d", p=P)[
                    :, t:J:NT, :]).then_inc(gathered[t], 16)
            for t in range(NT):
                sync.wait_ge(res_ready, t + 1)
                sync.dma_start(out[t * P:(t + 1) * P, :], h2[:, t, :]).then_inc(stored, 16)
            sync.wait_ge(stored, 16 * NT)

        @block.gpsimd
        def _(pool):
            steps = [0]

            def step(ins):
                steps[0] += 1
                ins.then_inc(pool_step, 1)
                pool.wait_ge(pool_step, steps[0])


            def rstd_of(n):
                for u in range(U):
                    pool.wait_ge(var_ready, U * n + u + 1)
                    nc.gpsimd.tensor_tensor(rstd[:, u * UT:(u + 1) * UT], ve[:, u * UT:(u + 1) * UT],
                                            cst[:, C_HALF:C_HALF + UT], ALU.pow).then_inc(rstd_ready, 1)

            pool.wait_ge(in_cst, 16)
            rstd_of(0)
            pool.wait_ge(in_rows, 16)
            pool.wait_ge(ln_ready, NT)
            nc.gpsimd.tensor_tensor(h[:], h[:], row[:, 1:2, :].to_broadcast([P, NT, D]), ALU.add).then_inc(hb_ready, 1)
            rstd_of(1)
            step(nc.gpsimd.tensor_tensor(rstd[:, NT:2 * NT], ve[:, NT:2 * NT], cst[:, C_HALF:C_HALF + NT], ALU.pow))
            pool.wait_ge(h2_ready, NT)
            for t in range(NT):
                ins = nc.gpsimd.tensor_scalar(xp[:, t, :], h2[:, t, :], mv[:, t, 0:1], rstd[:, NT + t:NT + t + 1],
                                              ALU.subtract, ALU.mult)
            step(ins)
            nc.gpsimd.tensor_tensor(xp[:], xp[:], row[:, 3:4, :].to_broadcast([P, NT, D]), ALU.add).then_inc(xpb_ready, 1)
            rstd_of(2)
            pool.wait_ge(part_act, 1)
            nc.gpsimd.tensor_tensor(left, xh[:], parts[:, 0, :, :], ALU.subtract).then_inc(part_pool, 1)
            pool.wait_ge(part_act, 2)
            pool.wait_ge(part_pool, 1)
            nc.gpsimd.tensor_tensor(parts[:, 2, :, :], left, parts[:, 1, :, :], ALU.subtract).then_inc(part_pool, 1)
            nc.gpsimd.tensor_tensor(h2[:], h2[:], x1[:], ALU.add).then_inc(base_ready, 1)
            pool.wait_ge(zero_rows, 16)
            for n in range(SENT):
                pool.wait_ge(put_ready, n + 1)
                pool.wait_ge(y_ready, n + 1)
                nc.gpsimd.indirect_dma_start(
                    out=choice_out, out_offset=bass.IndirectOffsetOnAxis(ap=put[:, n:n + 1], axis=0),
                    in_=y_rows[:, n, :], in_offset=None).then_inc(scattered, 16)

        @block.scalar
        def _(act):
            for i in range(PIECES):
                k = slice(i * KP // PIECES, (i + 1) * KP // PIECES)
                act.dma_start(tokw[:, k, :], tok_w[:, k, :]).then_inc(in_tok[i], 16)
            act.dma_start(cst[:], consts).then_inc(in_cst, 16)
            act.dma_start(ppt[:], pp).then_inc(in_small, 16)
            act.dma_start(qpt[:], qp).then_inc(in_small, 16)
            act.dma_start(spt[:], sp_par).then_inc(in_small, 16)
            act.dma_start(row[:], rows.partition_broadcast(P)).then_inc(in_rows, 16)
            act.wait_ge(zeros_ready, 1)
            nc.scalar.activation(sz[:, 0:1], zeros[0:SS, 0:1], ACT.Silu)
            act.wait_ge(in_cst, 16)
            nc.scalar.activation(cstb[:], cst[:, 0:C_BF], ACT.Copy).then_inc(cstb_ready, 1)

            for u in range(U):
                act.wait_ge(ln_T, 2 * u + 1)
                nc.scalar.activation(xT[:, 0, u * UN:(u + 1) * UN], bank[T_BANK[0][u][0]][0:HALF, 0:UN],
                                     ACT.Copy).then_inc(xT_act, 1)
            act.wait_ge(bcw_ready, 1)
            for m in range(KI):
                act.wait_ge(xz_acc, m + 1)
                nc.scalar.activation(conv[:, 0, m, :], bank[(6 + m) % 8][:], ACT.Identity,
                                     bias=ppt[:, PP_BIN + m:PP_BIN + m + 1]).then_inc(conv_in, 1)
                own = PP_CW + m * TAPS + TAPS - 1
                nc.scalar.activation(conv[:, 1, m, :], bank[(6 + m) % 8][:], ACT.Identity, scale=ppt[:, own:own + 1],
                                     bias=bcw[:, m:m + 1]).then_inc(conv_in, 1)
            act.wait_ge(xz_acc, KI + 1)
            for m in range(KI):
                act.wait_ge(conv_out, m + 1)
                nc.scalar.activation(xc[:, m, :], conv[:, 1, m, :], ACT.Silu,
                                     bias=ppt[:, PP_CB + m:PP_CB + m + 1]).then_inc(xc_ready, 1)
                if m == 0:
                    nc.scalar.activation(sz[:], bank[1][0:SS, :], ACT.Silu, bias=spt[0:SS, SP_Z:SP_Z + 1]).then_inc(
                        sz_ready, 1)
            act.wait_ge(xrep_acc, 1)
            nc.scalar.activation(xrep[SS:2 * SS, :], bank[3][SS:2 * SS, :], ACT.Copy).then_inc(xrep_ready, 1)
            act.wait_ge(st_acc, 1)
            act.wait_ge(small_ready, 2)
            nc.scalar.activation(decay[:], bank[2][0:SS, :], ACT.Sigmoid, scale=-1.0, bias=ndtb[:]).then_inc(decay_ready, 1)

            for t in range(NT):
                act.wait_ge(ssm_acc, t + 1)
                act.wait_ge(stats_ready, NT + t + 1)
                nc.scalar.activation(h2[:, t, :], bank[H2_BANK[t]][:, 0:D], ACT.Copy).then_inc(h2_ready, 1)

            for u in range(U):
                act.wait_ge(ln_T, 4 + 2 * u + 1)
                nc.scalar.activation(xT[:, 0, u * UN:(u + 1) * UN], bank[T_BANK[1][u][0]][0:HALF, 0:UN], ACT.Identity,
                                     scale=qpt[:, QP_L1W:QP_L1W + 1],
                                     bias=qpt[:, QP_L1B:QP_L1B + 1]).then_inc(xT_act, 1)
            act.wait_ge(qk_acc, 1)
            act.wait_ge(small_ready, 2)
            for a in range(2):
                nc.scalar.activation(qx[:, 0, :, a, :], bank[3][0:HALF, :].rearrange("p (b q) -> p b q", b=B),
                                     ACT.Identity, scale=hmask[:, a:a + 1], bias=qbm[:, a:a + 1]).then_inc(qx_act, 1)
            act.wait_ge(qk_acc, 4)
            nc.scalar.activation(kT[:, 1, :], bank[6][0:HALF, :], ACT.Identity,
                                 bias=qpt[:, QP_KB + 1:QP_KB + 2]).then_inc(kT_act, 1)

            def spread_probabilities(t):
                act.wait_ge(p_T, t + 1)
                for a in range(2):
                    nc.scalar.activation(px[:, t, :, a, :], pT(t), ACT.Copy, scale=bmask[:, a:a + 1]).then_inc(
                        px_act, 1)

            def outputs_of_even_heads(u):
                act.wait_ge(o_acc, u + 1)
                for i in range(IP):
                    nc.scalar.activation(o_half[:, u, i, :], bank[O_BANK[u][i]][0:HALF, 0:P], ACT.Copy,
                                         scale=bmask[0:HALF, 0:1]).then_inc(o_ready, 1)

            act.wait_ge(shifted, 1)
            nc.scalar.activation(prob[:, 0, :], prob[:, 0, :], ACT.Exp).then_inc(exp_ready, 1)
            for t in range(NT // U):
                spread_probabilities(t)
            act.wait_ge(shifted, 2)
            nc.scalar.activation(prob[:, 1, :], prob[:, 1, :], ACT.Exp).then_inc(exp_ready, 1)
            outputs_of_even_heads(0)
            spread_probabilities(NT - 1)
            outputs_of_even_heads(1)

            for u in range(U):
                act.wait_ge(ln_T, 8 + 2 * u + 1)
                nc.scalar.activation(xT[:, 0, u * UN:(u + 1) * UN], bank[T_BANK[2][u][0]][0:HALF, 0:UN], ACT.Identity,
                                     scale=qpt[:, QP_L2W:QP_L2W + 1],
                                     bias=qpt[:, QP_L2B:QP_L2B + 1]).then_inc(xT_act, 1)
            act.wait_ge(ln_ready, 3 * NT)
            nc.scalar.activation(parts[:, 0, :, :], xh[:], ACT.Copy).then_inc(part_act, 1)
            act.wait_ge(part_pool, 1)
            nc.scalar.activation(parts[:, 1, :, :], left, ACT.Copy).then_inc(part_act, 1)
            act.wait_ge(gap_ready, 1)
            for k in range(TOPK):
                nc.scalar.activation(wgt[:, k * NT:(k + 1) * NT], gap[:], ACT.Sigmoid,
                                     scale=(1.0, -1.0)[k]).then_inc(wgt_ready, 1)
            for e in range(E):
                for m in range(2):
                    act.wait_ge(fc_acc, 2 * e + m + 1)
                    if e >= HB:
                        act.wait_ge(pj_acc, QUAD + 1)
                    if e - HB >= QUAD:
                        act.wait_ge(pj_acc, len(OUTPUTS))
                    for n in range(KF // 2):
                        f = m * KF // 2 + n
                        nc.scalar.activation(
                            hid[:, e % HB, f, :], bank[2 * (e % 2) + m][:, n * CAP:(n + 1) * CAP], ACT.Gelu,
                            bias=ppt[:, PP_FCB + e * KF + f:PP_FCB + e * KF + f + 1]).then_inc(hid_ready, 1)

        @block.tensor
        def _(pe):
            mm = nc.tensor.matmul

            def keep_warm(to, n):
                for _ in range(n):
                    mm(to[:], zeros_b[:, 0:P], zeros_b[:], start=True, stop=True)

            def transpose_normalised(n, idle):
                for u in range(U):
                    if u == 1:
                        keep_warm(bank[(7, 3, 5)[n]], idle)
                    for c in range(2):
                        for i in range(UT):
                            t = u * UT + i
                            if c == 0:
                                pe.wait_ge(ln_ready, n * NT + t + 1)
                            ins = nc.tensor.transpose(bank[T_BANK[n][u][c]][0:HALF, i * P:(i + 1) * P],
                                                      xh[:, t, c * HALF:(c + 1) * HALF], ident)
                        ins.then_inc(ln_T, 1)

            def input_ready(n, u):
                pe.wait_ge(xT_act, U * n + u + 1)
                pe.wait_ge(xT_dve, U * n + u + 1)

            pe.wait_ge(zeros_ready, 1)
            keep_warm(bank[7], WARM[0])
            for i in range(PIECES - 2):
                pe.wait_ge(in_tok[i], 32)
                for t in range(NT):
                    mm(bank[t][:, 0:D], pat[:, i, t * P:(t + 1) * P], tokw[:, i, :], start=(i == 0), stop=False)
            pe.wait_ge(in_tok[PIECES - 2], 32)
            pe.wait_ge(in_tok[PIECES - 1], 32)
            for t in range(NT):
                for i in (PIECES - 2, PIECES - 1):
                    ins = mm(bank[t][:, 0:D], pat[:, i, t * P:(t + 1) * P], tokw[:, i, :],
                             start=False, stop=(i == PIECES - 1))
                ins.then_inc(tok_acc, 1)
            pe.wait_ge(in_cst, 16)
            keep_warm(bank[7], WARM[1])
            transpose_normalised(0, WARM[15])

            pe.wait_ge(in_ssm, 64)
            keep_warm(bank[7], WARM[2])
            for m in range(KI):
                for u in range(U):
                    n = slice(u * UN, (u + 1) * UN)
                    if m == 0:
                        input_ready(0, u)
                    for c in range(2):
                        ins = mm(bank[(6 + m) % 8][:, n], win[:, c, m * P:(m + 1) * P], xT[:, c, n], start=(c == 0),
                                 stop=(c == 1))
                ins.then_inc(xz_acc, 1)
            for c in range(2):
                ins = mm(bank[1][0:SS, :], winz[:, c, :], xT[:, c, :], start=(c == 0), stop=(c == 1))
            ins.then_inc(xz_acc, 1)
            keep_warm(bank[3], WARM[3])
            for k in range(KI):
                pe.wait_ge(xc_ready, k + 1)
                ins = mm(bank[2][:], wst[:, k, 0:2 * SS], xc[:, k, :], start=(k == 0), stop=(k == KI - 1))
                if k == KI - 1:
                    ins.then_inc(st_acc, 1)
                ins = mm(bank[3][0:(4 * SS if k == 0 else 3 * SS) - 2 * SS, :],
                         wst[:, k, 2 * SS:(4 * SS if k == 0 else 3 * SS)], xc[:, k, :], start=(k == 0),
                         stop=(k == KI - 1), skip_group_check=True)
                if k in (0, KI - 1):
                    ins.then_inc((xrep_acc, None, c_acc)[k], 1)
            pe.wait_ge(hb_ready, 1)
            for t in range(NT):
                mm(bank[H2_BANK[t]][:, 0:D], ident, h[:, t, :], start=True, stop=False)
            keep_warm(bank[1], WARM[4])
            pe.wait_ge(g_ready, 1)
            for t in range(NT):
                mm(bank[H2_BANK[t]][:, 0:D], cz[:, t * P:(t + 1) * P], wout[:], start=False, stop=True).then_inc(ssm_acc, 1)

            keep_warm(bank[3], WARM[5])
            transpose_normalised(1, WARM[16])
            keep_warm(bank[3], WARM[6])
            pe.wait_ge(in_attn, 48)
            def query_or_key(kind, c, u):
                at, n = kind * D + c * HALF, slice(u * UN, (u + 1) * UN)
                for k in range(2):
                    ins = mm(bank[3 + 2 * kind + c][0:HALF, n], qkvw[:, k, at:at + HALF], xT[:, k, n],
                             start=(k == 0), stop=(k == 1))
                if u == U - 1:
                    ins.then_inc(qk_acc, 1)

            def values(t):
                for k in range(2):
                    ins = mm(bank[(7, 0)[t // 2]][:, (t % 2) * D:(t % 2 + 1) * D], xT[:, k, t * P:(t + 1) * P],
                             qkvw[:, k, 2 * D:3 * D], start=(k == 0), stop=(k == 1))
                ins.then_inc(v_acc, 1)

            def scores(c, b):
                u, at = b // UB, c * UN + b % UB * T
                for i in range(PAIRS):
                    r = slice(i * PAIR, (i + 1) * PAIR)
                    ins = mm(bank[1 + u][r, at:at + T], qx[r, c, b, :, :].rearrange("p h q -> p (h q)"),
                             kT[r, c, b * T:(b + 1) * T], start=False, stop=(c == 1 and b % UB == UB - 1),
                             skip_group_check=True, tile_position=(i * PAIR, i * PAIR))
                if c == 1 and b % UB == UB - 1:
                    ins.then_inc(s_acc, 1)

            for kind in range(2):
                for u in range(U):
                    if kind == 0:
                        input_ready(1, u)
                    query_or_key(kind, 0, u)
            pe.wait_ge(cstb_ready, 1)
            for u in range(U):
                mm(bank[1 + u][0:HALF, :], cstb[0:HALF, C_ID:C_ID + HALF],
                   cstb[0:HALF, C_CM:C_CM + T].unsqueeze(1).to_broadcast([HALF, B, T]), start=True, stop=False,
                   skip_group_check=True)
            values(0)
            wide = {1: (0, 1, 0), 8: (0, 1, 1), 15: (1, 1, 0), 22: (1, 1, 1)}
            pe.wait_ge(qx_act, 2)
            pe.wait_ge(kT_dve, 1)
            for b in range(B):
                scores(0, b)
                if b in wide:
                    query_or_key(*wide[b])
                if b in IDLE0:
                    keep_warm(bank[0], 1)
            pe.wait_ge(qx_dve, 2)
            pe.wait_ge(kT_act, 1)
            for b in range(B):
                scores(1, b)
                if b in (3, 11, 19):
                    values((3, 11, 19).index(b) + 1)
                if b in IDLE1:
                    keep_warm(bank[3], 1)

            def transpose_probabilities(u):
                pe.wait_ge(prob_ready, u + 1)
                for t in range(u * UT, (u + 1) * UT):
                    for c in range(2):
                        at = c * UN + t % UT * P
                        ins = nc.tensor.transpose(bank[PT_BANK[t]][:, c * HALF:(c + 1) * HALF], prob[:, u, at:at + P],
                                                  ident[0:HALF, 0:HALF])
                    ins.then_inc(p_T, 1)

            def attend(u):
                for t in range(u * UT, (u + 1) * UT):
                    if t == NT - 2:
                        pe.wait_ge(px_dve, 1)
                    else:
                        pe.wait_ge(px_act, 2 * min(t + 1, NT - 1))
                for t in range(u * UT, (u + 1) * UT):
                    for pair in range(HEADS // 2):
                        c, g = pair // PAIRS, pair % PAIRS
                        for i in range(IP):
                            r = slice(i * PAIR, (i + 1) * PAIR)
                            if (pair, i) == (HEADS // 4, 0):
                                keep_warm(bank[(6, 3)[u]], WARM[14])
                            ins = mm(bank[O_BANK[u][i]][g * PAIR:(g + 1) * PAIR, 0:2 * P].rearrange(
                                         "p (h k n) -> p h k n", h=2, k=2 * UT)[:, :, t % UT * 2 + c, :],
                                     v[r, t, pair * PAIR:(pair + 1) * PAIR],
                                     px[r, t, 2 * pair:2 * pair + 2, :, :].rearrange("p h a q -> p h (a q)"),
                                     start=True, stop=True, tile_position=(i * PAIR, g * PAIR))
                ins.then_inc(o_acc, 1)

            def project_attention(u):
                pe.wait_ge(oT_ready, IP * (u + 1))
                for t in range(u * UT, (u + 1) * UT):
                    for k in range(2):
                        ins = mm(bank[X1_BANK[t]][:, 0:D], oT[:, 2 * t + k, :, :].rearrange("p i n -> p (i n)"), projw[:, k, :],
                                 start=(k == 0), stop=(k == 1))
                    ins.then_inc(x1_acc, 1)

            keep_warm(bank[3], WARM[10])
            transpose_probabilities(0)
            pe.wait_ge(v_ready, 2)
            keep_warm(bank[3], WARM[11])
            attend(0)
            keep_warm(bank[6], WARM[12])
            transpose_probabilities(1)
            project_attention(0)
            keep_warm(bank[1], WARM[13])
            attend(1)
            keep_warm(bank[3], WARM[19])
            project_attention(1)

            keep_warm(bank[1], WARM[7])
            transpose_normalised(2, WARM[17])
            for t in range(NT):
                if t % UT == 0:
                    input_ready(2, t // UT)
                for k in range(2):
                    for j in range(QUAD):
                        at = t * P + j * REST
                        ins = mm(bank[3][j * REST:(j + 1) * REST, t * E:(t + 1) * E], xT[:, k, at:at + REST],
                                 gatew[:, k, :], start=(k == 0), stop=(k == 1), tile_position=(0, j * REST))
            ins.then_inc(lg_acc, 1)
            keep_warm(bank[4], WARM[8])
            pe.wait_ge(hotb_ready, 1)
            flat = hotb[:, :, :].rearrange("p j e -> p (j e)")
            mm(bank[4][:, 0:J * E], cstb[:, C_TRI:C_TRI + P], flat, start=True, stop=False, skip_group_check=True)
            for j in range(J - 1):
                ins = mm(bank[4][:, (j + 1) * E:J * E], cstb[:, C_ONE:C_ONE + P],
                         hotb[:, j:j + 1, :].to_broadcast([P, J - 1 - j, E]), start=False, stop=(j == J - 2),
                         skip_group_check=True)
            ins.then_inc(pos_acc, 1)

            def dispatch(e):
                to = bank[5 + e % 2]
                if e >= 2:
                    pe.wait_ge(xbT_ready, 2 * (e - 1))
                    pe.wait_ge(put_sum, 2 * (e - 1))
                pe.wait_ge(oh_ready, NT * (e + 1))
                if e == E - QUAD:
                    pe.wait_ge(share_ready, 1)
                for c in range(2):
                    for part in range(PARTS):
                        if e == 0 and c == 0:
                            pe.wait_ge(*((part_act, 1), (part_act, 2), (part_pool, 2))[part])
                        for t in range(NT):
                            ins = mm(to[0:HALF, c * CAP:(c + 1) * CAP], parts[:, part, t, c * HALF:(c + 1) * HALF],
                                     oh[:, e % 2, t, :], start=(part == 0 and t == 0),
                                     stop=(part == PARTS - 1 and t == NT - 1))
                j = e % QUAD
                at = 2 * CAP
                for t in range(NT):
                    mm(to[:, at:at + 3], oh[:, e % 2, t, 0:P], token[:, t, e, :], start=(t == 0), stop=(t == NT - 1))
                for t in range(NT):
                    ins = mm(to[j * REST:(j + 1) * REST, at + 4:at + 7], oh[:, e % 2, t, P:CAP], token[:, t, e, :],
                             start=(t == 0), stop=(t == NT - 1), tile_position=(0, j * REST))
                if e >= E - QUAD:
                    for t in range(NT):
                        ins = mm(to[j * REST:(j + 1) * REST, at + 12:at + 12 + PARTS], oh[:, e % 2, t, P:CAP],
                                 share_part[:, :, t, j], start=(t == 0), stop=(t == NT - 1),
                                 tile_position=(0, j * REST))
                if e == E - 1:
                    for t in range(NT):
                        ins = mm(to[:, at + 8:at + 8 + PARTS], oh[:, e % 2, t, 0:P], share_part[:, :, t, j],
                                 start=(t == 0), stop=(t == NT - 1))
                ins.then_inc(xb_acc, 1)

            def hidden(e):
                pe.wait_ge(xbT_ready, 2 * (e + 1))
                pe.wait_ge(in_fc[e], 16)
                if e >= 2:
                    pe.wait_ge(hid_ready, KF * (e - 1))
                for f in range(KF):
                    to = bank[2 * (e % 2) + f // (KF // 2)][:, f % (KF // 2) * CAP:(f % (KF // 2) + 1) * CAP]
                    for c in range(2):
                        ins = mm(to, fcw[:, e, c, f * P:(f + 1) * P], xbT[:, e % 2, c, :], start=(c == 0), stop=(c == 1))
                    if f % (KF // 2) == KF // 2 - 1:
                        ins.then_inc(fc_acc, 1)

            def project(n):
                first_e, last_e = OUTPUTS[n]
                to = bank[(4, 7)[n % 2]]
                for e in range(first_e, last_e + 1):
                    pe.wait_ge(in_pj[e], 16)
                if n >= 2:
                    pe.wait_ge(y_ready, n - 1)
                for f in range(KF):
                    pe.wait_ge(hid_ready, KF * last_e + f + 1)
                    if first_e == last_e:
                        ins = mm(to[:, 0:D], hid[:, first_e % HB, f, 0:P], pjw[:, first_e, f, :],
                                 start=(f == 0), stop=(f == KF - 1))
                    else:
                        for j in range(QUAD):
                            e = first_e + j
                            ins = mm(to[j * REST:(j + 1) * REST, 0:D], hid[:, e % HB, f, P:CAP], pjw[:, e, f, :],
                                     start=(f == 0), stop=(f == KF - 1), tile_position=(0, j * REST))
                ins.then_inc(pj_acc, 1)

            keep_warm(bank[3], WARM[18])
            pe.wait_ge(token_ready, 1)
            dispatch(0)
            dispatch(1)
            for e in range(E):
                hidden(e)
                if e + 2 < E:
                    dispatch(e + 2)
                for n, (_, last_e) in enumerate(OUTPUTS):
                    if last_e == e:
                        project(n)
            pe.wait_ge(comb_ready, 2)
            for n in range(2):
                pe.wait_ge(y_ready, SENT + n + 1)
                for t in range(NT):
                    ins = mm(bank[t][:, 0:D], comb[:, n, t * P:(t + 1) * P], y_rows[:, SENT + n, :],
                             start=(n == 0), stop=(n == 1))
                    if n == 1:
                        ins.then_inc(comb_acc, 1)

        @block.vector
        def _(dve):
            V = nc.vector
            steps, sums = [0], [0]

            def step(ins):
                steps[0] += 1
                ins.then_inc(dve_step, 1)
                dve.wait_ge(dve_step, steps[0])

            def layer_norm(n, src, added, summed=None, affine=None, first_early=False):
                def statistics(u):
                    g = slice(u * UT, (u + 1) * UT)
                    for t in range(u * UT, (u + 1) * UT):
                        added(t)
                        ins = V.bn_stats(st[:, t, :], summed(t) if summed else src[:, t, :])
                        ins.then_inc(stats_ready, 1)
                    dve.wait_ge(stats_ready, n * NT + (u + 1) * UT)
                    for t in range(u * UT, (u + 1) * UT):
                        ins = V.bn_aggr(mv[:, t, :], st[:, t, :])
                    step(ins)
                    if summed:
                        V.tensor_scalar(ve[:, NT + u * UT:NT + (u + 1) * UT], mv[:, g, 1], EPS, None, ALU.add)
                        V.tensor_scalar(ve[:, g], mv[:, g, 1], 1.0 + EPS, EPS * EPS, ALU.mult,
                                        ALU.add).then_inc(var_ready, 1)
                    else:
                        V.tensor_scalar(ve[:, g], mv[:, g, 1], EPS, None, ALU.add).then_inc(var_ready, 1)

                def normalised(u):
                    dve.wait_ge(rstd_ready, U * n + u + 1)
                    if summed:
                        dve.wait_ge(h2_ready, (u + 1) * UT)
                    for t in range(u * UT, (u + 1) * UT):
                        V.tensor_scalar(xh[:, t, :], src[:, t, :], mv[:, t, 0:1], rstd[:, t:t + 1],
                                        ALU.subtract, ALU.mult).then_inc(ln_ready, 1)

                def transposed(u):
                    dve.wait_ge(ln_T, 2 * (U * n + u) + 2)
                    to, at = xT[:, 1, u * UN:(u + 1) * UN], bank[T_BANK[n][u][1]][0:HALF, 0:UN]
                    if affine is None:
                        V.tensor_copy(to, at).then_inc(xT_dve, 1)
                    else:
                        V.tensor_scalar(to, at, qpt[:, affine[0] + 1:affine[0] + 2], qpt[:, affine[1] + 1:affine[1] + 2],
                                        ALU.mult, ALU.add).then_inc(xT_dve, 1)

                statistics(0)
                if first_early:
                    outputs_of_odd_heads(1)
                    normalised(0)
                    statistics(1)
                    transposed(0)
                else:
                    statistics(1)
                    normalised(0)
                normalised(1)
                if not first_early:
                    transposed(0)
                return transposed

            V.memset(zeros[:], 0.0).then_inc(zeros_ready, 1)

            dve.wait_ge(in_rows, 16)
            def add_b(t):
                dve.wait_ge(tok_acc, t + 1)
                V.tensor_tensor(h[:, t, :], bank[t][:, 0:D], row[:, 0, :], ALU.add).then_inc(h_ready, 1)
                dve.wait_ge(h_ready, t + 1)

            last_transposed = layer_norm(0, h, add_b)
            dve.wait_ge(in_small, 48)
            dve.wait_ge(in_cst, 16)
            V.tensor_scalar(ndtb[:], spt[0:SS, SP_DT:SP_DT + 1], -1.0, None, ALU.mult).then_inc(small_ready, 1)
            cw = ppt[:, PP_CW:PP_CW + KI * TAPS].rearrange("p (m s) -> p m s", m=KI)[:, :, TAPS - 1]
            V.tensor_tensor(bcw[:], ppt[:, PP_BIN:PP_BIN + KI], cw, ALU.mult).then_inc(bcw_ready, 1)
            last_transposed(1)
            V.tensor_scalar(qbm[:], hmask, qpt[:, QP_QB:QP_QB + 1], None, ALU.mult).then_inc(small_ready, 1)

            for m in range(KI):
                dve.wait_ge(conv_in, 2 * (m + 1))
                tap = PP_CW + m * TAPS
                xv = conv[:, 0, m, :].rearrange("p (b t) -> p b t", b=B)
                sv = conv[:, 1, m, :].rearrange("p (b t) -> p b t", b=B)
                for s in range(1, TAPS):
                    ins = V.scalar_tensor_tensor(sv[:, :, s:T], xv[:, :, 0:T - s], ppt[:, tap + TAPS - 1 - s:tap + TAPS - s],
                                                 sv[:, :, s:T], ALU.mult, ALU.add)
                    if s < TAPS - 1:
                        step(ins)
                ins.then_inc(conv_out, 1)
            dve.wait_ge(xrep_ready, 1)
            dve.wait_ge(st_acc, 1)
            V.scalar_tensor_tensor(bx[:], bank[2][SS:2 * SS, :], spt[SS:2 * SS, SP_DT:SP_DT + 1], xrep[SS:2 * SS, :],
                                   ALU.add, ALU.mult)
            dve.wait_ge(decay_ready, 1)
            step(V.memset(decay[:].rearrange("p (b t) -> p b t", b=B)[:, :, 0:1], 0.0))
            step(V.tensor_tensor_scan(hs, decay[:], bx[:], 0.0, ALU.mult, ALU.add))
            dve.wait_ge(c_acc, 1)
            dve.wait_ge(sz_ready, 1)
            step(V.scalar_tensor_tensor(cz[:], bank[3][0:SS, :], spt[0:SS, SP_C:SP_C + 1], sz[:], ALU.add, ALU.mult))
            V.tensor_tensor(cz[:], hs, cz[:], ALU.mult).then_inc(g_ready, 1)

            layer_norm(1, h2, lambda t: dve.wait_ge(ssm_acc, t + 1), lambda t: bank[H2_BANK[t]][:, 0:D],
                       (QP_L1W, QP_L1B))(1)

            dve.wait_ge(qk_acc, 2)
            V.tensor_scalar(kT[:, 0, :], bank[5][0:HALF, :], qpt[:, QP_KB:QP_KB + 1], None, ALU.add).then_inc(kT_dve, 1)
            dve.wait_ge(qk_acc, 3)
            for a in range(2):
                V.tensor_scalar(qx[:, 1, :, a, :], bank[4][0:HALF, :].rearrange("p (b q) -> p b q", b=B),
                                qpt[:, QP_QB + 1:QP_QB + 2], hmask[:, a:a + 1], ALU.add, ALU.mult).then_inc(qx_dve, 1)
            def copy_values(g):
                dve.wait_ge(v_acc, 2 * g + 2)
                V.tensor_tensor(v[:, 2 * g:2 * g + 2, :], bank[(7, 0)[g]][:, 0:2 * D].rearrange(
                    "p (t d) -> p t d", t=2), row[:, 2:3, :].to_broadcast([P, 2, D]), ALU.add).then_inc(v_ready, 1)

            def shift(u):
                dve.wait_ge(s_acc, u + 1)
                scores = bank[1 + u][0:HALF, :].rearrange("p (b k) -> p b k", k=T)
                step(V.tensor_reduce(top_score[:], scores, AX_X, ALU.max))
                V.tensor_tensor(prob[:, u, :].rearrange("p (b k) -> p b k", k=T), scores,
                                top_score[:].unsqueeze(2).to_broadcast([HALF, 2 * UB, T]), ALU.subtract).then_inc(
                                    shifted, 1)

            def normalise(u):
                dve.wait_ge(exp_ready, u + 1)
                weights = prob[:, u, :].rearrange("p (b k) -> p b k", k=T)
                step(V.tensor_reduce(total[:, u, :], weights, AX_X, ALU.add))
                step(V.reciprocal(total[:, u, :], total[:, u, :]))
                V.tensor_tensor(weights, weights, total[:, u, :].unsqueeze(2).to_broadcast([HALF, 2 * UB, T]),
                                ALU.mult).then_inc(prob_ready, 1)

            def outputs_of_odd_heads(u):
                for i in range(IP):
                    dve.wait_ge(o_ready, IP * u + i + 1)
                    V.scalar_tensor_tensor(oT[:, u * 2 * UT:(u + 1) * 2 * UT, i, :],
                                           bank[O_BANK[u][i]][0:HALF, P:2 * P].rearrange("p (k n) -> p k n", k=2 * UT),
                                           bmask[0:HALF, 1:2],
                                           o_half[:, u, i, :].rearrange("p (k n) -> p k n", k=2 * UT), ALU.mult, ALU.add).then_inc(oT_ready, 1)

            copy_values(0)
            shift(0)
            copy_values(1)
            normalise(0)
            shift(1)
            normalise(1)
            outputs_of_odd_heads(0)
            dve.wait_ge(p_T, NT - 1)
            V.tensor_tensor(px[:, NT - 2, :, :, :],
                            pT(NT - 2).unsqueeze(2).to_broadcast([P, HEADS, 2, T]),
                            bmask.unsqueeze(1).unsqueeze(3).to_broadcast([P, HEADS, 2, T]), ALU.mult).then_inc(px_dve, 1)
            dve.wait_ge(xpb_ready, 1)

            def add_attention(t):
                dve.wait_ge(x1_acc, t + 1)
                V.tensor_tensor(x1[:, t, :], bank[X1_BANK[t]][:, 0:D], xp[:, t, :], ALU.add).then_inc(x1_ready, 1)
                dve.wait_ge(x1_ready, t + 1)

            layer_norm(2, x1, add_attention, None, (QP_L2W, QP_L2B), True)(1)

            dve.wait_ge(lg_acc, 1)
            for t in range(NT):
                ins = V.max(top[:, t, :], bank[3][:, t * E:(t + 1) * E])
            step(ins)
            for t in range(NT):
                ins = V.max_index(chosen[:, t, :], top[:, t, :], bank[3][:, t * E:(t + 1) * E])
            step(ins)
            for k in range(TOPK):
                ins = V.tensor_tensor(hotb[:, k * NT:(k + 1) * NT, :],
                                      cst[:, C_CHOICE:C_CHOICE + NT * E].rearrange("p (t e) -> p t e", t=NT),
                                      chosen[:, :, k:k + 1].to_broadcast([P, NT, E]), ALU.is_equal)
            ins.then_inc(hotb_ready, 1)
            V.tensor_tensor(gap[:], top[:, :, 0], top[:, :, 1], ALU.subtract).then_inc(gap_ready, 1)
            dve.wait_ge(hotb_ready, 1)
            V.scalar_tensor_tensor(token[:, :, :, 2], hotb[:, NT:J, :], float(N), token[:, :, :, 2],
                                   ALU.mult, ALU.add).then_inc(token_ready, 1)
            step(V.tensor_tensor(miss[:], hotb[:, 0:NT, :], hotb[:, NT:J, :], ALU.add))
            step(V.tensor_scalar(miss[:], miss[:], -NOWHERE, NOWHERE, ALU.mult, ALU.add))
            dve.wait_ge(pos_acc, 1)
            step(V.tensor_tensor(pos[:], bank[4][:, 0:J * E].rearrange("p (j e) -> p j e", j=J), hotb[:], ALU.mult))
            step(V.tensor_tensor(place[:], pos[:, 0:NT, :], pos[:, NT:J, :], ALU.add))
            step(V.tensor_tensor(place[:], place[:], miss[:], ALU.add))

            def one_hot(e):
                if e >= 2:
                    dve.wait_ge(xb_acc, e - 1)
                for t in range(NT):
                    V.tensor_scalar(oh[:, e % 2, t, :], cstb[:, C_SLOT:C_SLOT + CAP], place[:, t, e:e + 1], None,
                                    ALU.is_equal).then_inc(oh_ready, 1)

            def affine(e):
                dve.wait_ge(xb_acc, e + 1)
                if e >= 2:
                    dve.wait_ge(fc_acc, 2 * (e - 1))
                for c in range(2):
                    V.tensor_scalar(xbT[:, e % 2, c, :], bank[5 + e % 2][0:HALF, c * CAP:(c + 1) * CAP],
                                    qpt[:, QP_L2W + c:QP_L2W + c + 1], qpt[:, QP_L2B + c:QP_L2B + c + 1],
                                    ALU.mult, ALU.add).then_inc(xbT_ready, 1)

            def rows_of_slots(e):
                j = e % QUAD
                to = bank[5 + e % 2]
                for n, r, at in ((OUTPUTS.index((e, e)), slice(0, P), 2 * CAP),
                                 (OUTPUTS.index((e - j, e - j + QUAD - 1)), slice(j * REST, (j + 1) * REST), 2 * CAP + 4)):
                    if n >= SENT:
                        V.tensor_reduce(slot_share[r, n - SENT:n - SENT + 1],
                                        to[r, at + 8:at + 8 + PARTS], AX_X, ALU.add)
                    V.tensor_copy(row_of[r, n, 0:3], to[r, at:at + 3]).then_inc(put_sum, 1)
                    sums[0] += 1
                    dve.wait_ge(put_sum, sums[0])
                    step(V.scalar_tensor_tensor(row_of[r, n, 3:4], row_of[r, n, 1:2], cst[r, C_NHOLE + n:C_NHOLE + n + 1],
                                                row_of[r, n, 0:1], ALU.mult, ALU.add))
                    if n < SENT:
                        ins = V.scalar_tensor_tensor(put[r, n:n + 1], row_of[r, n, 2:3], cst[r, C_HOLE + n:C_HOLE + n + 1],
                                                     row_of[r, n, 3:4], ALU.add, ALU.add)
                        if r.stop - r.start == P or j == QUAD - 1:
                            ins.then_inc(put_ready, 1)
                    else:
                        step(V.scalar_tensor_tensor(slot_token[r, n - SENT:n - SENT + 1], row_of[r, n, 2:3],
                                                    cst[r, C_HOLE + n:C_HOLE + n + 1], row_of[r, n, 3:4],
                                                    ALU.add, ALU.add))

            def slots_by_token(n):
                step(V.tensor_scalar(row_of[:, SENT + n, 0:1], slot_token[:, n:n + 1], float(N), -float(N),
                                     ALU.is_ge, ALU.mult))
                step(V.tensor_tensor(slot_token[:, n:n + 1], slot_token[:, n:n + 1], row_of[:, SENT + n, 0:1], ALU.add))
                for t in range(NT):
                    ins = V.tensor_scalar(in_tile[:, n, t:t + 1], slot_token[:, n:n + 1], -float(t * P), None, ALU.add)
                step(ins)
                for t in range(NT):
                    ins = V.tensor_scalar(comb[:, n, t * P:(t + 1) * P], cst[:, C_SLOT:C_SLOT + P], in_tile[:, n, t:t + 1],
                                          slot_share[:, n:n + 1], ALU.is_equal, ALU.mult)
                ins.then_inc(comb_ready, 1)

            def split_shares():
                dve.wait_ge(wgt_ready, 2)
                for k, to in enumerate((share, share2)):
                    ins = V.tensor_tensor(to[:], hotb[:, k * NT:(k + 1) * NT, E - QUAD:E],
                                          wgt[:, k * NT:(k + 1) * NT].unsqueeze(2).to_broadcast([P, NT, QUAD]), ALU.mult)
                step(ins)
                step(V.tensor_tensor(share[:], share[:], share2[:], ALU.add))
                for part in range(PARTS - 1):
                    step(V.tensor_copy(share_part[:, part, :, :], share[:]))
                    step(V.tensor_tensor(share[:], share[:], share_part[:, part, :, :], ALU.subtract))
                V.tensor_copy(share_part[:, PARTS - 1, :, :], share[:]).then_inc(share_ready, 1)

            def outputs(n):
                dve.wait_ge(pj_acc, n + 1)
                first_e, last_e = OUTPUTS[n]
                own = first_e if first_e == last_e else E + first_e // QUAD
                V.tensor_tensor(y_rows[:, n, :], bank[(4, 7)[n % 2]][:, 0:D], pjb[:, own, :], ALU.add).then_inc(y_ready, 1)

            one_hot(0)
            one_hot(1)
            affine(0)
            one_hot(2)
            rows_of_slots(0)
            affine(1)
            rows_of_slots(1)
            split_shares()
            dve.wait_ge(in_pjb, 16 * (E + 1))
            for e in range(E - 1):
                if 0 < e < E - 2:
                    one_hot(e + 2)
                for n, (_, last_e) in enumerate(OUTPUTS):
                    if last_e == e - 1:
                        outputs(n)
                if e + 2 < E:
                    affine(e + 2)
                    rows_of_slots(e + 2)
            for n in range(2):
                slots_by_token(n)
            for n, (_, last_e) in enumerate(OUTPUTS):
                if last_e == E - 2:
                    outputs(n)
            dve.wait_ge(base_ready, 1)
            outputs(SENT)

            def add_choice(k, t):
                if k == 0:
                    dve.wait_ge(gathered[t], 16)
                else:
                    dve.wait_ge(choice_added, t + 1)
                V.scalar_tensor_tensor(h2[:, t, :], got[:, k * NT + t, :], wgt[:, k * NT + t:k * NT + t + 1], h2[:, t, :],
                                       ALU.mult, ALU.add).then_inc(choice_added, 1)

            for t in range(NT):
                add_choice(0, t)
            for t in range(NT - 3):
                add_choice(1, t)
            outputs(SENT + 1)
            for t in range(NT - 3, NT):
                add_choice(1, t)
            for t in range(NT):
                dve.wait_ge(choice_added, NT + t + 1)
                dve.wait_ge(comb_acc, t + 1)
                V.tensor_tensor(h2[:, t, :], bank[t][:, 0:D], h2[:, t, :], ALU.add).then_inc(res_ready, 1)


def kernel(x, L0_tok_W, L0_tok_b, L0_attn_W_in, L0_attn_b_in, L0_attn_conv_w, L0_attn_conv_b, L0_attn_W_x,
           L0_attn_b_x, L0_attn_W_dt, L0_attn_b_dt, L0_attn_W_out, L0_attn_b_out, L0_ffn_ln1_w, L0_ffn_ln1_b,
           L0_ffn_ln2_w, L0_ffn_ln2_b, L0_ffn_attn_qkv_w, L0_ffn_attn_qkv_b, L0_ffn_attn_proj_w,
           L0_ffn_attn_proj_b, L0_ffn_w_g, L0_ffn_exp_fc_w, L0_ffn_exp_fc_b, L0_ffn_exp_proj_w,
           L0_ffn_exp_proj_b):
    import concourse.bacc as bacc
    from concourse.bass_utils import run_bass_kernel_spmd

    def a(v):
        return np.asarray(v)

    def halves(w):
        return a(w).reshape(2, HALF, -1).transpose(1, 0, 2)

    def chunks(w):
        w = a(w)
        return w.reshape(w.shape[0] // P, P, -1).transpose(1, 0, 2)

    def by_j(w):
        return np.tile(w, S)

    def by_i(w):
        return np.repeat(w, S, axis=-1)

    side = x.shape[-1] // 4
    patches = a(x).reshape(B, 3, 4, side, 4, side).transpose(3, 5, 1, 0, 2, 4).reshape(PIX, N)
    b_dt, b_x, b_in = a(L0_attn_b_dt), a(L0_attn_b_x), a(L0_attn_b_in)
    w_x, qkv_b = a(L0_attn_W_x), a(L0_ffn_attn_qkv_b)
    pp = np.concatenate([
        b_in[:INNER].reshape(KI, P).T,
        a(L0_attn_conv_w).reshape(KI, P, TAPS).transpose(1, 0, 2).reshape(P, KI * TAPS),
        a(L0_attn_conv_b).reshape(KI, P).T,
        a(L0_ffn_exp_fc_b).reshape(E, KF, P).transpose(2, 0, 1).reshape(P, E * KF)], axis=1)
    qp = np.concatenate([a(v).reshape(2, HALF).T for v in (
        L0_ffn_ln1_w, L0_ffn_ln1_b, L0_ffn_ln2_w, L0_ffn_ln2_b, qkv_b[:D], qkv_b[D:2 * D])], axis=1)
    state_b = np.stack([
        np.concatenate([by_j(b_dt[:S]), by_j(b_x[2 * S:3 * S])]),
        np.concatenate([by_j(b_x[3 * S:4 * S])] * 2),
        np.concatenate([by_i(b_in[INNER:WIN])] * 2)], axis=1)
    data = {
        "patches": patches.reshape(KP, P, N).transpose(1, 0, 2),
        "tok_w": chunks(a(L0_tok_W).T),
        "w_in": halves(a(L0_attn_W_in)[:, :INNER]),
        "w_z": halves(by_i(a(L0_attn_W_in)[:, INNER:WIN])),
        "w_state": chunks(np.concatenate([by_j(a(L0_attn_W_dt)[:, :S]), by_j(w_x[:, 2 * S:3 * S]),
                                          by_j(w_x[:, 3 * S:4 * S]), by_i(np.eye(INNER, S, dtype=w_x.dtype))],
                                         axis=1)),
        "w_out": np.repeat(a(L0_attn_W_out)[:S], S, axis=0),
        "qkv_w": halves(L0_ffn_attn_qkv_w),
        "proj_w": halves(L0_ffn_attn_proj_w),
        "gate_w": halves(L0_ffn_w_g),
        "fc_w": a(L0_ffn_exp_fc_w).reshape(E, 2, HALF, F).transpose(2, 0, 1, 3),
        "pj_w": a(L0_ffn_exp_proj_w).reshape(E, KF, P, D).transpose(2, 0, 1, 3),
        "pp": pp,
        "qp": qp,
        "sp_par": state_b,
        "rows": np.stack([a(L0_tok_b), a(L0_attn_b_out), qkv_b[2 * D:], a(L0_ffn_attn_proj_b)]),
        "pj_b": a(L0_ffn_exp_proj_b).reshape(E, D),
        "consts": constants(),
    }
    nc = bacc.Bacc("TRN2", target_bir_lowering=False, num_devices=1)
    arrays, args = {}, []
    for name, v in data.items():
        v = np.ascontiguousarray(v)
        arrays[f"in_{name}"] = v
        args.append(nc.dram_tensor(f"in_{name}", v.shape, mybir.dt.from_np(v.dtype), kind="ExternalInput").ap())
    args.append(nc.dram_tensor("out_0_dram", (N, D), F32, kind="ExternalOutput").ap())
    vit_block(nc, *args)
    r = run_bass_kernel_spmd(nc, [arrays], core_ids=[0])
    return r.results[0]["out_0_dram"].reshape(B, T, D)
```
